# Optimizing a Trainium2 kernel written in Bass

```python
import numpy as np
import jax
import jax.numpy as jnp

def _softmax(x, axis=-1):
    return jax.nn.softmax(x, axis=axis)

def _gelu(x):
    return jax.nn.gelu(x, approximate=True)

def _silu(x):
    return jax.nn.silu(x)

def _sigmoid(x):
    return jax.nn.sigmoid(x)

def _layernorm(x, axis=-1, eps=1e-05):
    m = jnp.mean(x, axis=axis, keepdims=True)
    v = jnp.var(x, axis=axis, keepdims=True)
    return (x - m) / jnp.sqrt(v + eps)

def _scatter_add(tgt, idx, src, axis=0):
    return tgt.at[idx].add(src)

def _segment_sum(src, seg, n):
    return jax.ops.segment_sum(src, seg, n)
kernel_name = 'mk_xattn_ffn_d1_seqx_r8_a2aa6d'

def setup_inputs(seed: int=0):
    np.random.seed(seed)
    _w = jnp.asarray

    def _rec_inputs():
        import jax
        import jax.numpy as jnp
        _rk = jax.random.key(seed)
        x = -0.0005207 + 1.001 * jax.random.normal(jax.random.fold_in(_rk, 1), (32, 64, 512), jnp.float32)
        _lenS = 64 - jax.random.randint(jax.random.fold_in(_rk, 7), (32,), 0, max(1, 64 // 4) + 1, jnp.int32)
        _lenS2 = 64 - jax.random.randint(jax.random.fold_in(_rk, 8), (32,), 0, max(1, 64 // 4) + 1, jnp.int32)
        _ctx_4096P = jax.random.normal(jax.random.fold_in(_rk, 11), (32, 16, 512), jnp.float32)
        _ctx_4096c = jax.random.dirichlet(jax.random.fold_in(_rk, 511), 0.3 * jnp.ones((16,), jnp.float32), (32, 64))
        _ctx_4096t = jnp.einsum('bsk,bkd->bsd', _ctx_4096c, _ctx_4096P)
        _ctx_4096t = _ctx_4096t * jax.lax.rsqrt(jnp.mean(jnp.square(_ctx_4096t)) + 1e-12) * 0.953939
        ctx_4096 = -0.00010331 + 0.999899 * (_ctx_4096t + 0.3 * jax.random.normal(jax.random.fold_in(_rk, 611), (32, 64, 512), jnp.float32))
        return (x, ctx_4096)
    x, ctx_4096 = _rec_inputs()

    def _L0_xattn_setup():
        import jax, jax.numpy as jnp
        import numpy as np
        import math
        HIDDEN = 512
        N_HEADS = 32
        HEAD_DIM = 128
        N_KV_HEADS = 4
        N_GROUPS = N_HEADS // N_KV_HEADS
        key = jax.random.key(seed)
        ks = jax.random.split(key, 6)
        B, NL, S = (8, 64, 512)
        latents = jax.random.normal(ks[0], (B, NL, HIDDEN), dtype=jnp.float32)
        context = jax.random.normal(ks[1], (B, S, HIDDEN), dtype=jnp.float32)
        scale = 1.0 / math.sqrt(HIDDEN)
        Wq = jax.random.normal(ks[2], (HIDDEN, N_HEADS * HEAD_DIM), dtype=jnp.float32) * scale
        Wk = jax.random.normal(ks[3], (HIDDEN, N_KV_HEADS * HEAD_DIM), dtype=jnp.float32) * scale
        Wv = jax.random.normal(ks[4], (HIDDEN, N_KV_HEADS * HEAD_DIM), dtype=jnp.float32) * scale
        Wo = jax.random.normal(ks[5], (N_HEADS * HEAD_DIM, HIDDEN), dtype=jnp.float32) * scale
        return {'latents': latents, 'context': context, 'Wq': Wq, 'Wk': Wk, 'Wv': Wv, 'Wo': Wo}
    _L0_xattn_all = _L0_xattn_setup()
    _L0_xattn_in = {k: v for k, v in _L0_xattn_all.items() if k in ('Wq', 'Wk', 'Wv', 'Wo')}
    del _L0_xattn_all

    def _L0_ffn_setup():
        import jax, jax.numpy as jnp
        import numpy as np
        DIM = 512
        INTER = 1792
        SPARSITY = 32
        RANK = 16
        key = jax.random.key(seed)
        ks = jax.random.split(key, 5)
        B, T = (32, 1)
        x = jax.random.normal(ks[0], (B, T, DIM), dtype=jnp.float32)
        c1_w = jax.random.normal(ks[1], (RANK, DIM), dtype=jnp.float32) * (1.0 / np.sqrt(DIM))
        c2_w = jax.random.normal(ks[2], (INTER, RANK), dtype=jnp.float32) * (1.0 / np.sqrt(RANK))
        w1 = jax.random.normal(ks[3], (INTER, DIM), dtype=jnp.float32) * (1.0 / np.sqrt(DIM))
        w2t = jax.random.normal(ks[4], (INTER, DIM), dtype=jnp.float32) * (1.0 / np.sqrt(INTER))
        return {'x': x, 'c1_w': c1_w, 'c2_w': c2_w, 'w1': w1, 'w2t': w2t}
    _L0_ffn_all = _L0_ffn_setup()
    _L0_ffn_in = {k: v for k, v in _L0_ffn_all.items() if k in ('c1_w', 'c2_w', 'w1', 'w2t')}
    del _L0_ffn_all
    return {'x': x, 'ctx_4096': ctx_4096, 'L0_xattn_Wq': _L0_xattn_in['Wq'], 'L0_xattn_Wk': _L0_xattn_in['Wk'], 'L0_xattn_Wv': _L0_xattn_in['Wv'], 'L0_xattn_Wo': _L0_xattn_in['Wo'], 'L0_ffn_c1_w': _L0_ffn_in['c1_w'], 'L0_ffn_c2_w': _L0_ffn_in['c2_w'], 'L0_ffn_w1': _L0_ffn_in['w1'], 'L0_ffn_w2t': _L0_ffn_in['w2t']}

def reference(x, ctx_4096, L0_xattn_Wq, L0_xattn_Wk, L0_xattn_Wv, L0_xattn_Wo, L0_ffn_c1_w, L0_ffn_c2_w, L0_ffn_w1, L0_ffn_w2t):
    import jax
    import jax.numpy as jnp

    def _L0_xattn_ref(latents, context, Wq, Wk, Wv, Wo):
        import jax, jax.numpy as jnp
        import numpy as np
        import math
        HIDDEN = 512
        N_HEADS = 32
        HEAD_DIM = 128
        N_KV_HEADS = 4
        N_GROUPS = N_HEADS // N_KV_HEADS
        b, q_len, _ = latents.shape
        kv_len = q_len + context.shape[1]
        hidden_states = jnp.concatenate([context, latents], axis=1)
        q = (latents @ Wq).reshape(b, q_len, N_KV_HEADS, N_GROUPS, HEAD_DIM)
        k = (hidden_states @ Wk).reshape(b, kv_len, N_KV_HEADS, HEAD_DIM)
        v = (hidden_states @ Wv).reshape(b, kv_len, N_KV_HEADS, HEAD_DIM)
        scale = 1.0 / math.sqrt(HEAD_DIM)
        scores = jnp.einsum('bqhgd,bkhd->bhgqk', q, k) * scale
        attn = jax.nn.softmax(scores.astype(jnp.float32), axis=-1).astype(q.dtype)
        out = jnp.einsum('bhgqk,bkhd->bqhgd', attn, v)
        out = out.reshape(b, q_len, N_HEADS * HEAD_DIM)
        return out @ Wo

    def _L0_ffn_ref(x, c1_w, c2_w, w1, w2t):
        import jax, jax.numpy as jnp
        import numpy as np
        DIM = 512
        INTER = 1792
        SPARSITY = 32
        RANK = 16
        B, T, M = x.shape
        xf = x.reshape(B * T, M)
        inter = xf @ c1_w.T @ c2_w.T
        n_blocks = INTER // SPARSITY
        blk = inter.reshape(B * T, n_blocks, SPARSITY)
        idx = jnp.argmax(blk, axis=-1) + jnp.arange(0, INTER, SPARSITY)
        w1_g = w1[idx]
        w2_g = w2t[idx]
        h = jax.nn.relu(jnp.einsum('bkm,bm->bk', w1_g, xf))
        out = jnp.einsum('bk,bkm->bm', h, w2_g)
        return out.reshape(B, T, M)
    x = x + _L0_xattn_ref(_layernorm(x, axis=-1), ctx_4096, L0_xattn_Wq, L0_xattn_Wk, L0_xattn_Wv, L0_xattn_Wo)
    x = x + _L0_ffn_ref(_layernorm(x, axis=-1), L0_ffn_c1_w, L0_ffn_c2_w, L0_ffn_w1, L0_ffn_w2t)
    return x

_drawn_inputs = setup_inputs


def setup_inputs(seed=0):
    import zlib

    import numpy as np

    out = dict(_drawn_inputs(seed))
    spreads = {}
    factors = {}
    for name, (base, spread) in spreads.items():
        noise = np.random.default_rng([zlib.crc32(name.encode()), seed]).standard_normal(out[name].shape)
        drawn = base * np.exp(spread * noise) if base else spread * noise
        out[name] = jnp.asarray(drawn.astype(out[name].dtype))
    for name, factor in factors.items():
        out[name] = (out[name] * factor).astype(out[name].dtype)
    return out
```

```python
from contextlib import ExitStack

import concourse.bass as bass
from concourse import mybir

F32 = mybir.dt.float32
F32R = mybir.dt.float32r
BF16 = mybir.dt.bfloat16
ALU = mybir.AluOpType
ACT = mybir.ActivationFunctionType
AXIS = mybir.AxisListType

P = 128
B, L, D = 32, 64, 512
HEADS, GROUPS, DH = 32, 4, 128
HG = HEADS // GROUPS
KEYS = 2 * L
KC = D // P
TOKENS = B * L
INTER, SPARSE = 1792, 32
NI = INTER // P
EPS = 1e-5

KT = 4
NKT = B // KT
TB = 8
TT = TB * L
NT = B // TB
TC = TT // P
FN = 448
FQ = INTER // FN
FB = FN // SPARSE
RANK = 16
RANK_STEP = 32


def wait(engine, semaphore, value):
    if isinstance(value, int) and value <= 0:
        return
    engine.wait_ge(semaphore, value)


class Names:

    def __init__(self, nc, stack, phase):
        self.nc, self.stack, self.phase = nc, stack, phase

    def sb(self, name, shape, dtype=F32):
        return self.stack.enter_context(self.nc.sbuf_tensor(f"{self.phase}_{name}", shape, dtype))

    def ps(self, name, shape=(P, 512), dtype=F32):
        return self.stack.enter_context(self.nc.psum_tensor(f"{self.phase}_{name}", list(shape), dtype))

    def sem(self, name):
        return self.stack.enter_context(self.nc.semaphore(f"{self.phase}_{name}"))


def three_passes(nc, out, stationary, moving, start, stop):
    (sh, sl), (mh, ml) = stationary, moving
    nc.tensor.matmul(out, sh, mh, start=start, stop=False)
    nc.tensor.matmul(out, sh, ml, start=False, stop=False)
    return nc.tensor.matmul(out, sl, mh, start=False, stop=stop)


def inverse_root(nc, dve, var, std, guess, step, out, done, before):
    nc.vector.reciprocal(guess[:], std[:]).then_inc(done, 1)
    dve.wait_ge(done, before + 1)
    nc.vector.tensor_tensor(step[:, 0], guess[:], guess[:], ALU.mult).then_inc(done, 1)
    dve.wait_ge(done, before + 2)
    nc.vector.scalar_tensor_tensor(step[:, 1], var[:], -0.5, step[:, 0], ALU.mult, ALU.mult).then_inc(done, 1)
    dve.wait_ge(done, before + 3)
    nc.vector.scalar_tensor_tensor(out[:], step[:, 1], 1.5, guess[:], ALU.add, ALU.mult).then_inc(done, 1)
    dve.wait_ge(done, before + 4)


def project_keys_values(nc, x, ctxT, wk, wv, kT_d, v_d, xnT_d):
    with ExitStack() as stack:
        n = Names(nc, stack, "kv")
        ident = n.sb("ident", [P, P])
        w_raw = n.sb("w_raw", [P, 2, KC, D])
        w = n.sb("w", [P, 2, 2, KC, D], F32R)
        x_in = n.sb("x_in", [P, 2, 2, D])
        c_in = n.sb("c_in", [P, 2, KC, KT * L])
        xn = n.sb("xn", [P, 2, D])
        stats = n.sb("stats", [P, 2, 6])
        meanvar = n.sb("meanvar", [P, 2, 2])
        std = n.sb("std", [P, 2])
        var = n.sb("var", [P, 2])
        guess = n.sb("guess", [P, 2])
        step = n.sb("step", [P, 2, 2])
        rstd = n.sb("rstd", [P, 2])
        spacer = n.sb("spacer", [P, 1])
        h = n.sb("h", [P, 2, 2, KC, KT, KEYS], F32R)
        k_out = n.sb("k_out", [P, 2, GROUPS, KT * KEYS])
        v_out = n.sb("v_out", [P, 2, 2, GROUPS, KT, DH], F32R)
        xT = [n.ps(f"xT{i}", (P, 2, KT * L)) for i in range(2)]
        proj = [n.ps(f"proj{i}") for i in range(4)]

        ident_set = n.sem("ident_set")
        ident_done = n.sem("ident_done")
        w_in = n.sem("w_in")
        w_high = n.sem("w_high")
        w_low = n.sem("w_low")
        x_loaded = [n.sem(f"x_loaded{i}") for i in range(2)]
        c_loaded = [n.sem(f"c_loaded{i}") for i in range(2)]
        stats_done = n.sem("stats_done")
        meanvar_done = n.sem("meanvar_done")
        std_done = n.sem("std_done")
        var_done = n.sem("var_done")
        rstd_step = n.sem("rstd_step")
        xn_done = n.sem("xn_done")
        xT_done = n.sem("xT_done")
        xT_high = n.sem("xT_high")
        xT_low = n.sem("xT_low")
        c_high = n.sem("c_high")
        c_low = n.sem("c_low")
        k_done = n.sem("k_done")
        v_done = n.sem("v_done")
        k_copied = n.sem("k_copied")
        v_high = n.sem("v_high")
        v_low = n.sem("v_low")
        k_stored = [n.sem(f"k_stored{i}") for i in range(2)]
        v_stored = [n.sem(f"v_stored{i}") for i in range(2)]
        x_stored = [n.sem(f"x_stored{i}") for i in range(2)]

        x_rows = x.rearrange("(i r p) d -> i p r d", r=2, p=P)
        c_cols = ctxT.rearrange("(c p) (i n) -> i p c n", p=P, i=NKT)

        def tiles(engine, body):
            for p in range(2):
                body(0, p)
            with engine.Fori(1, NKT // 2 - 1) as pair:
                for p in range(2):
                    body(pair, p)
            for p in range(2):
                body(NKT // 2 - 1, p)

        def following(pair, p):
            if p == 0:
                return pair, 1
            return None if isinstance(pair, int) and pair == NKT // 2 - 1 else (pair + 1, 0)

        block = stack.enter_context(nc.Block())

        @block.sync
        def _(sp):
            def load(pair, p):
                i = 2 * pair + p
                wait(sp, xn_done, i - 1)
                sp.dma_start(x_in[:, p], x_rows[i]).then_inc(x_loaded[p], 16)
                wait(sp, c_low, i - 1)
                sp.dma_start(c_in[:, p], c_cols[i]).then_inc(c_loaded[p], 16)

            load(0, 0)
            for s, src in enumerate((wk, wv)):
                sp.dma_start(w_raw[:, s], src.rearrange("(c p) n -> p c n", p=P)).then_inc(w_in, 16)
            load(0, 1)

            def body(pair, p):
                i = 2 * pair + p
                if isinstance(pair, int) and pair == NKT // 2 - 1:
                    pass
                else:
                    load(pair + 1, p)
                for part in range(2):
                    wait(sp, xT_low, 2 * i + 2)
                    sp.dma_start(xnT_d[part, pair, :, :, p], h[:, p, part, :, :, L:].bitcast(F32)).then_inc(x_stored[p], 16)
                wait(sp, k_copied, GROUPS * (i + 1))
                sp.dma_start(kT_d[:, :, i].rearrange("g p n -> p g n"), k_out[:, p]).then_inc(k_stored[p], 16)
                wait(sp, v_low, KT * (i + 1))
                for part in range(2):
                    sp.dma_start(v_d[:, part, :, i].rearrange("g p n d -> p g (n d)"),
                                 v_out[:, p, part].rearrange("p g n d -> p g (n d)").bitcast(F32)).then_inc(v_stored[p], 16)

            tiles(sp, body)
            for p in range(2):
                sp.wait_ge(x_stored[p], 16 * NKT)
                sp.wait_ge(k_stored[p], 16 * NKT // 2)
                sp.wait_ge(v_stored[p], 16 * NKT)

        @block.gpsimd
        def _(pool):
            nc.gpsimd.memset(ident[:], 1.0).then_inc(ident_set, 1)
            pool.wait_ge(ident_set, 1)
            nc.gpsimd.affine_select(out=ident[:], in_=ident[:], compare_op=ALU.is_equal, fill=0.0, base=0,
                                    pattern=[[-1, P]], channel_multiplier=1).then_inc(ident_done, 1)

            def split(pair, p):
                i = 2 * pair + p
                pool.wait_ge(c_high, i + 1)
                for c in range(2):
                    last = nc.gpsimd.tensor_tensor(h[:, p, 1, 2 * c:2 * c + 2, :, 0:L],
                                                   c_in[:, p, 2 * c:2 * c + 2].rearrange("p c (n t) -> p c n t", n=KT),
                                                   h[:, p, 0, 2 * c:2 * c + 2, :, 0:L], ALU.subtract)
                last.then_inc(c_low, 1)

            def body(pair, p):
                after = following(pair, p)
                if after:
                    split(*after)

            split(0, 0)
            tiles(pool, body)

        @block.scalar
        def _(act):
            def prepare(pair, p):
                i = 2 * pair + p
                act.wait_ge(var_done, i + 1)
                nc.scalar.activation(std[:], var[:], ACT.Sqrt).then_inc(std_done, 1)
                act.wait_ge(c_loaded[p], 16 * (pair + 1))
                wait(act, v_done, KT * (i - 1))
                wait(act, x_stored[p], 32 * pair)
                nc.scalar.activation(h[:, p, 0, :, :, 0:L],
                                     c_in[:, p].rearrange("p c (n t) -> p c n t", n=KT), ACT.Copy).then_inc(c_high, 1)

            def split(pair, p):
                i = 2 * pair + p
                act.wait_ge(xT_done, i + 1)
                for c in range(2):
                    nc.scalar.activation(h[:, p, 0, 2 * c:2 * c + 2, :, L:],
                                         xT[c][:].rearrange("p c (n t) -> p c n t", n=KT), ACT.Copy).then_inc(xT_high, 1)

            def body(pair, p):
                i = 2 * pair + p
                after = following(pair, p)
                if after:
                    prepare(*after)
                wait(act, k_stored[p], 16 * pair)
                for g in range(GROUPS):
                    act.wait_ge(k_done, GROUPS * i + g + 1)
                    nc.scalar.activation(k_out[:, p, g], proj[g][:], ACT.Copy).then_inc(k_copied, 1)
                if after:
                    split(*after)
                wait(act, v_stored[p], 32 * pair)
                for b in range(KT):
                    act.wait_ge(v_done, KT * i + b + 1)
                    nc.scalar.activation(v_out[:, p, 0, :, b], proj[b][:].rearrange("p (g d) -> p g d", g=GROUPS),
                                         ACT.Copy).then_inc(v_high, 1)

            act.wait_ge(w_in, 32)
            for s in range(2):
                nc.scalar.activation(w[:, s, 0], w_raw[:, s], ACT.Copy).then_inc(w_high, 1)
            prepare(0, 0)
            split(0, 0)
            tiles(act, body)

        @block.vector
        def _(dve):
            def layer_norm(pair, p):
                i = 2 * pair + p
                dve.wait_ge(x_loaded[p], 16 * (pair + 1))
                for r in range(2):
                    last = nc.vector.bn_stats(stats[:, r], x_in[:, p, r])
                last.then_inc(stats_done, 1)
                dve.wait_ge(stats_done, i + 1)
                wait(dve, std_done, i)
                nc.vector.memset(spacer[:], 0.0)
                for r in range(2):
                    last = nc.vector.bn_aggr(meanvar[:, r], stats[:, r])
                last.then_inc(meanvar_done, 1)
                dve.wait_ge(meanvar_done, i + 1)
                nc.vector.tensor_scalar(var[:], meanvar[:, :, 1], EPS, None, ALU.add).then_inc(var_done, 1)
                dve.wait_ge(std_done, i + 1)
                inverse_root(nc, dve, var, std, guess, step, rstd, rstd_step, 4 * i)
                wait(dve, xT_done, i)
                for r in range(2):
                    last = nc.vector.tensor_scalar(xn[:, r], x_in[:, p, r], meanvar[:, r, 0:1], rstd[:, r:r + 1],
                                                   ALU.subtract, ALU.mult)
                last.then_inc(xn_done, 1)

            def split(pair, p):
                i = 2 * pair + p
                for c in range(2):
                    dve.wait_ge(xT_high, 2 * i + c + 1)
                    nc.vector.tensor_tensor(h[:, p, 1, 2 * c:2 * c + 2, :, L:],
                                            xT[c][:].rearrange("p c (n t) -> p c n t", n=KT),
                                            h[:, p, 0, 2 * c:2 * c + 2, :, L:], ALU.subtract).then_inc(xT_low, 1)

            def body(pair, p):
                i = 2 * pair + p
                after = following(pair, p)
                if after:
                    layer_norm(*after)
                    split(*after)
                for b in range(KT):
                    dve.wait_ge(v_high, KT * i + b + 1)
                    nc.vector.tensor_tensor(v_out[:, p, 1, :, b], proj[b][:].rearrange("p (g d) -> p g d", g=GROUPS),
                                            v_out[:, p, 0, :, b], ALU.subtract).then_inc(v_low, 1)

            layer_norm(0, 0)
            for s in range(2):
                dve.wait_ge(w_high, s + 1)
                nc.vector.tensor_tensor(w[:, s, 1], w_raw[:, s], w[:, s, 0], ALU.subtract).then_inc(w_low, 1)
            split(0, 0)
            tiles(dve, body)

        @block.tensor
        def _(pe):
            def transpose(pair, p):
                i = 2 * pair + p
                pe.wait_ge(xn_done, i + 1)
                wait(pe, xT_low, 2 * i)
                for c in range(KC):
                    for r in range(2):
                        last = nc.tensor.transpose(xT[c // 2][:, c % 2, r * P:(r + 1) * P],
                                                   xn[:, r, c * P:(c + 1) * P], ident[:])
                last.then_inc(xT_done, 1)

            def body(pair, p):
                i = 2 * pair + p
                pe.wait_ge(xT_low, 2 * i + 2)
                pe.wait_ge(c_low, i + 1)
                for g in range(GROUPS):
                    wait(pe, v_low, KT * (i - 1) + g + 1)
                    for c in range(KC):
                        last = three_passes(nc, proj[g][:],
                                            [w[:, 0, s, c, g * DH:(g + 1) * DH] for s in range(2)],
                                            [h[:, p, s, c].rearrange("p n t -> p (n t)") for s in range(2)],
                                            c == 0, c == KC - 1)
                    last.then_inc(k_done, 1)
                after = following(pair, p)
                if after:
                    transpose(*after)
                for b in range(KT):
                    pe.wait_ge(k_copied, GROUPS * i + b + 1)
                    for c in range(KC):
                        last = three_passes(nc, proj[b][:], [h[:, p, s, c, b] for s in range(2)],
                                            [w[:, 1, s, c] for s in range(2)], c == 0, c == KC - 1)
                    last.then_inc(v_done, 1)

            pe.wait_ge(ident_done, 1)
            transpose(0, 0)
            pe.wait_ge(w_low, 2)
            tiles(pe, body)


def attend(nc, x, wq, wo, kT_d, v_d, xnT_d, x1_d):
    with ExitStack() as stack:
        n = Names(nc, stack, "at")
        ident = n.sb("ident", [P, P])
        xT = n.sb("xT", [P, 2, 2, KC, TT], F32R)
        wq_raw = n.sb("wq_raw", [P, 2, KC, DH])
        wq_s = n.sb("wq_s", [P, 2, 2, KC, DH], F32R)
        wo_raw = n.sb("wo_raw", [P, 2, D])
        wo_s = n.sb("wo_s", [P, 2, 2, D], F32R)
        q = n.sb("q", [P, 2, TB, HG, L])
        k = n.sb("k", [P, 2, TB, KEYS])
        v = n.sb("v", [P, 2, 2, TB, DH], F32R)
        negmax = n.sb("negmax", [P, 4])
        total = n.sb("total", [P, 4])
        inverse = n.sb("inverse", [P, 4])
        e = n.sb("e", [P, 4, KEYS])
        prob = n.sb("prob", [P, 4, KEYS])
        probT = n.sb("probT", [P, 2, 512], F32R)
        o = n.sb("o", [P, 2, 2, HG, TT], F32R)
        x1 = n.sb("x1", [P, TC, D])
        q_ps = n.ps("q_ps")
        s_ps = n.ps("s_ps", (P, 4, KEYS))
        pT_ps = n.ps("pT_ps")
        o_ps = n.ps("o_ps")
        acc = [n.ps(f"acc{c}") for c in range(TC)]

        ident_set = n.sem("ident_set")
        ident_done = n.sem("ident_done")
        xT_loaded = [n.sem(f"xT_loaded{i}") for i in range(2)]
        wq_loaded = [n.sem(f"wq_loaded{i}") for i in range(2)]
        wo_loaded = [n.sem(f"wo_loaded{i}") for i in range(2)]
        k_loaded = [n.sem(f"k_loaded{i}") for i in range(2)]
        v_loaded = [n.sem(f"v_loaded{i}") for i in range(2)]
        x_loaded = n.sem("x_loaded")
        x1_stored = n.sem("x1_stored")
        wq_high = n.sem("wq_high")
        wq_low = n.sem("wq_low")
        wo_high = n.sem("wo_high")
        wo_low = n.sem("wo_low")
        q_done = n.sem("q_done")
        q_copied = n.sem("q_copied")
        s_done = n.sem("s_done")
        max_done = n.sem("max_done")
        e_done = n.sem("e_done")
        inverse_done = n.sem("inverse_done")
        prob_done = n.sem("prob_done")
        pT_done = n.sem("pT_done")
        pT_high = n.sem("pT_high")
        pT_low = n.sem("pT_low")
        pv_done = n.sem("pv_done")
        o_high = n.sem("o_high")
        o_low = n.sem("o_low")
        wo_done = n.sem("wo_done")
        acc_read = n.sem("acc_read")

        x_rows = x.rearrange("(t c p) d -> t p c d", c=TC, p=P)

        def rounds(engine, body):
            for g in range(GROUPS):
                body(0, g, True, g >= 1, g >= 2)
            with engine.Fori(1, NT) as T:
                for g in range(GROUPS):
                    body(T, g, True, True, True)
            body(NT, 0, False, True, True)
            body(NT, 1, False, False, True)

        def earlier(T, g, steps):
            return (T, g - steps) if g >= steps else (T - 1, g - steps + GROUPS)

        def next_wo(T, g, j, c):
            first = isinstance(T, int) and (T, g, j) == (0, 1, 7)
            last = isinstance(T, int) and (T, g, j) == (NT, 1, 7)
            if last or not (c or first):
                return None
            number = HG * (GROUPS * T + g - 2) + j + 1
            head_group = (g - 2) % GROUPS if j < 7 else (g - 1) % GROUPS
            return number, head_group, (j + 1) % 8

        block = stack.enter_context(nc.Block())

        @block.sync
        def _(sp):
            def body(T, g, a, b, c):
                u = GROUPS * T + g
                for j in range(HG):
                    slot = HG * u + j
                    if a and j == 0 and g == 0:
                        load_xT(T, 0)
                    if a and j == 4 and g == 0:
                        load_xT(T, 1)
                    if a:
                        wait(sp, wq_low, slot - 1)
                        sp.dma_start(wq_raw[:, j % 2], wq[:, HG * g + j]).then_inc(wq_loaded[j % 2], 16)
                    after = next_wo(T, g, j, c)
                    if after:
                        number, wg, head = after
                        wait(sp, wo_low, number - 1)
                        row = (HG * wg + head) * DH
                        sp.dma_start(wo_raw[:, head % 2], wo[row:row + DH]).then_inc(wo_loaded[head % 2], 16)
                    if a and j == 4:
                        wait(sp, pv_done, TB * (u - 1))
                        sp.dma_start(k[:, g % 2].rearrange("p (i n) t -> p i (n t)", i=2),
                                     kT_d[g, :, bass.ds(2 * T, 2)]).then_inc(k_loaded[g % 2], 16)
                        for part in range(2):
                            sp.dma_start(v[:, g % 2, part].bitcast(F32).rearrange("p (i n) d -> p i (n d)", i=2),
                                         v_d[g, part, :, bass.ds(2 * T, 2)].rearrange("p i n d -> p i (n d)")
                                         ).then_inc(v_loaded[g % 2], 16)
                    if a and j == 6 and g == 2:
                        wait(sp, x1_stored, 16 * T)
                        sp.dma_start(x1[:], x_rows[T]).then_inc(x_loaded, 16)

            def load_xT(T, half):
                u = GROUPS * T + 2 * half
                wait(sp, q_done, HG * (u - 2))
                for part in range(2):
                    sp.dma_start(xT[:, half, part].bitcast(F32).rearrange("p c n -> p (c n)"),
                                 xnT_d[part, T].rearrange("p c i n t -> p (c i n t)")).then_inc(xT_loaded[half], 16)

            rounds(sp, body)

        @block.gpsimd
        def _(pool):
            nc.gpsimd.memset(ident[:], 1.0).then_inc(ident_set, 1)
            pool.wait_ge(ident_set, 1)
            nc.gpsimd.affine_select(out=ident[:], in_=ident[:], compare_op=ALU.is_equal, fill=0.0, base=0,
                                    pattern=[[-1, P]], channel_multiplier=1).then_inc(ident_done, 1)

            def body(T, g, a, b, c):
                u = GROUPS * T + g
                for j in range(HG):
                    if a:
                        pool.wait_ge(wq_high, HG * u + j + 1)
                        nc.gpsimd.tensor_tensor(wq_s[:, j % 2, 1], wq_raw[:, j % 2], wq_s[:, j % 2, 0],
                                                ALU.subtract).then_inc(wq_low, 1)
                    after = next_wo(T, g, j, c)
                    if after:
                        number, _, head = after
                        pool.wait_ge(wo_high, number + 1)
                        nc.gpsimd.tensor_tensor(wo_s[:, head % 2, 1], wo_raw[:, head % 2], wo_s[:, head % 2, 0],
                                                ALU.subtract).then_inc(wo_low, 1)

            rounds(pool, body)

        @block.scalar
        def _(act):
            def finish_batch(T, g, j):
                u = GROUPS * T + g
                number = TB * u + j
                act.wait_ge(pv_done, number + 1)
                if j == 0:
                    wait(act, wo_done, HG * (u - 1))
                nc.scalar.activation(o[:, g % 2, 0, :, j * L:(j + 1) * L],
                                     o_ps[:].rearrange("p (h t) -> p h t", h=HG), ACT.Copy).then_inc(o_high, 1)

            def high_probT(T, g, j):
                number = TB * (GROUPS * T + g) + j
                act.wait_ge(pT_done, number + 1)
                wait(act, pv_done, number)
                nc.scalar.activation(probT[:, 0], pT_ps[:], ACT.Copy).then_inc(pT_high, 1)

            def body(T, g, a, b, c):
                u = GROUPS * T + g
                for j in range(HG):
                    slot = HG * u + j
                    bT, bg = earlier(T, g, 1)
                    before = (bT, bg, j - 1) if j else (*earlier(T, g, 2), HG - 1)
                    has_before = b if j else c
                    if has_before:
                        high_probT(*before)
                    if a:
                        act.wait_ge(wq_loaded[j % 2], 16 * (4 * u + j // 2 + 1))
                        wait(act, q_done, slot - 1)
                        nc.scalar.activation(wq_s[:, j % 2, 0], wq_raw[:, j % 2], ACT.Copy).then_inc(wq_high, 1)
                    if b:
                        batch = slot - HG
                        act.wait_ge(max_done, batch + 1)
                        wait(act, prob_done, batch)
                        for i in range(4):
                            last = nc.scalar.activation(e[:, i], s_ps[:, i], ACT.Exp, bias=negmax[:, i:i + 1],
                                                        accum_out=total[:, i:i + 1])
                        last.then_inc(e_done, 1)
                    if has_before:
                        finish_batch(*before)
                    after = next_wo(T, g, j, c)
                    if after:
                        number, _, head = after
                        act.wait_ge(wo_loaded[head % 2], 16 * (number // 2 + 1) if isinstance(number, int)
                                    else 16 * (4 * (u - 2) + (j + 1) // 2 + 1))
                        wait(act, wo_done, number - 1)
                        nc.scalar.activation(wo_s[:, head % 2, 0], wo_raw[:, head % 2], ACT.Copy).then_inc(wo_high, 1)
                    if a:
                        act.wait_ge(q_done, slot + 1)
                        if j == 0:
                            wait(act, s_done, TB * (u - 1))
                        nc.scalar.activation(q[:, g % 2, :, j], q_ps[:].rearrange("p (n t) -> p n t", n=TB),
                                             ACT.Copy, scale=DH ** -0.5).then_inc(q_copied, 1)
                    if c and g == 2 and j == 1 and not (isinstance(T, int) and T == 0):
                        store_x1(T)

            def store_x1(T):
                act.wait_ge(acc_read, TC * T)
                act.dma_start(x1_d[T - 1], x1[:]).then_inc(x1_stored, 16)

            rounds(act, body)
            store_x1(NT)
            act.wait_ge(x1_stored, 16 * NT)

        @block.vector
        def _(dve):
            def low_probT(T, g, j):
                number = TB * (GROUPS * T + g) + j
                dve.wait_ge(pT_high, number + 1)
                nc.vector.tensor_tensor(probT[:, 1], pT_ps[:], probT[:, 0], ALU.subtract).then_inc(pT_low, 1)

            def low_o(T, g, j):
                number = TB * (GROUPS * T + g) + j
                dve.wait_ge(o_high, number + 1)
                part = o[:, g % 2, :, :, j * L:(j + 1) * L]
                nc.vector.tensor_tensor(part[:, 1], o_ps[:].rearrange("p (h t) -> p h t", h=HG), part[:, 0],
                                        ALU.subtract).then_inc(o_low, 1)

            def body(T, g, a, b, c):
                u = GROUPS * T + g
                for j in range(HG):
                    batch = HG * (u - 1) + j
                    bT, bg = earlier(T, g, 1)
                    before = (bT, bg, j - 1) if j else (*earlier(T, g, 2), HG - 1)
                    has_before = b if j else c
                    if has_before:
                        low_probT(*before)
                    if b:
                        dve.wait_ge(s_done, batch + 1)
                        wait(dve, e_done, batch)
                        nc.vector.tensor_reduce(negmax[:], s_ps[:], AXIS.X, ALU.max, negate=True).then_inc(max_done, 1)
                        dve.wait_ge(e_done, batch + 1)
                        wait(dve, prob_done, batch)
                        nc.vector.reciprocal(inverse[:], total[:]).then_inc(inverse_done, 1)
                        dve.wait_ge(inverse_done, batch + 1)
                        wait(dve, pT_done, batch)
                        nc.vector.tensor_tensor(prob[:], e[:], inverse[:].unsqueeze(2).to_broadcast([P, 4, KEYS]),
                                                ALU.mult).then_inc(prob_done, 1)
                    if has_before:
                        low_o(*before)
                if c and g == 1 and not (isinstance(T, int) and T == 0):
                    dve.wait_ge(x_loaded, 16 * T)
                    for i in range(TC):
                        dve.wait_ge(wo_done, HG * (u - 1) if i == TC - 1 else HG * (u - 1))
                        nc.vector.tensor_tensor(x1[:, i], x1[:, i], acc[i][:], ALU.add).then_inc(acc_read, 1)

            rounds(dve, body)

        @block.tensor
        def _(pe):
            def times_v(T, g, j):
                u = GROUPS * T + g
                number = TB * u + j
                pe.wait_ge(pT_low, number + 1)
                if j == 0:
                    pe.wait_ge(v_loaded[g % 2], 32 * (2 * T + g // 2 + 1))
                wait(pe, o_low, number)
                three_passes(nc, o_ps[:], [v[:, g % 2, s, j] for s in range(2)],
                             [probT[:, s] for s in range(2)], True, True).then_inc(pv_done, 1)

            def body(T, g, a, b, c):
                u = GROUPS * T + g
                bT, bg = earlier(T, g, 1)
                _, cg = earlier(T, g, 2)
                for j in range(HG):
                    slot = HG * u + j
                    batch = slot - HG
                    if b:
                        if j == 0:
                            pe.wait_ge(q_copied, HG * u)
                            pe.wait_ge(k_loaded[bg % 2], 16 * (2 * bT + bg // 2 + 1))
                        wait(pe, e_done, batch)
                        for i in range(4):
                            last = nc.tensor.matmul(s_ps[:, i],
                                                    q[:, bg % 2, j, 2 * i:2 * i + 2].rearrange("p h t -> p (h t)"),
                                                    k[:, bg % 2, j], start=True, stop=True)
                        last.then_inc(s_done, 1)
                    if j and b:
                        times_v(bT, bg, j - 1)
                    if j == 0 and c:
                        times_v(*earlier(T, g, 2), HG - 1)
                    if c:
                        number = slot - 2 * HG
                        pe.wait_ge(wo_low, number + 1)
                        if j == 0 and cg == 0:
                            wait(pe, acc_read, TC * (T if g >= 2 else T - 1))
                        for i in range(TC):
                            if j == 0 and i == 0:
                                pe.wait_ge(o_low, HG * (u - 1) - 1)
                            if j == 0 and i == TC - 1:
                                pe.wait_ge(o_low, HG * (u - 1))
                            last = three_passes(nc, acc[i][:],
                                                [o[:, cg % 2, s, j, i * P:(i + 1) * P] for s in range(2)],
                                                [wo_s[:, j % 2, s] for s in range(2)],
                                                cg == 0 and j == 0, cg == GROUPS - 1 and j == HG - 1)
                        last.then_inc(wo_done, 1)
                    if a:
                        pe.wait_ge(wq_low, slot + 1)
                        wait(pe, q_copied, slot)
                        if j == 0 and g % 2 == 0:
                            pe.wait_ge(xT_loaded[g // 2], 32 * (T + 1))
                        for i in range(KC):
                            last = three_passes(nc, q_ps[:], [wq_s[:, j % 2, s, i] for s in range(2)],
                                                [xT[:, g // 2, s, i] for s in range(2)], i == 0, i == KC - 1)
                        last.then_inc(q_done, 1)
                    if b:
                        pe.wait_ge(prob_done, batch + 1)
                        wait(pe, pT_low, batch)
                        for i in range(4):
                            last = nc.tensor.transpose(pT_ps[:, i * P:(i + 1) * P], prob[:, i], ident[:])
                        last.then_inc(pT_done, 1)

            pe.wait_ge(ident_done, 1)
            rounds(pe, body)


def feed_forward(nc, x1_d, c1, c2, w1, w2, out):
    with ExitStack() as stack:
        n = Names(nc, stack, "ff")
        ident = n.sb("ident", [P, P])
        ident_bf = n.sb("ident_bf", [P, P], BF16)
        rank = n.sb("rank", [P, SPARSE])
        rank_bf = n.sb("rank_bf", [P, SPARSE], BF16)
        c1_s = n.sb("c1_s", [P, 2, KC, P], F32R)
        c2_s = n.sb("c2_s", [P, INTER], F32R)
        raw = n.sb("raw", [P, 2, 512])
        w1_s = n.sb("w1_s", [P, NI, 2, KC, P], F32R)
        w2_s = n.sb("w2_s", [P, NI, 2, D], F32R)
        x_ln = n.sb("x_ln", [P, TC, D])
        x_res = raw
        stats = n.sb("stats", [P, TC, 6])
        meanvar = n.sb("meanvar", [P, TC, 2])
        var = n.sb("var", [P, TC])
        std = n.sb("std", [P, TC])
        guess = n.sb("guess", [P, TC])
        step = n.sb("step", [P, 2, TC])
        rstd = n.sb("rstd", [P, TC])
        spacer = n.sb("spacer", [P, 1])
        xT = n.sb("xT", [P, 2, KC, TT], F32R)
        t_s = n.sb("t_s", [P, TT], F32R)
        top = n.sb("top", [P, 2, FB])
        leader = n.sb("leader", [P, INTER // SPARSE], BF16)
        mask = n.sb("mask", [P, TC, INTER], BF16)
        hidden = n.sb("hidden", [P, NI, TT])
        used_s = n.sb("used_s", [P, 2, 2, TT], F32R)

        acc = [n.ps(f"acc{c}") for c in range(TC)]
        h_ps = [n.ps(f"h{i}") for i in range(2)]
        m_ps = [n.ps(f"m{i}") for i in range(2)]

        ident_set = n.sem("ident_set")
        ident_done = n.sem("ident_done")
        ident_bf_done = n.sem("ident_bf_done")
        rank_done = n.sem("rank_done")
        rank_bf_done = n.sem("rank_bf_done")
        w_high = n.sem("w_high")
        w_low = n.sem("w_low")
        x_ln_loaded = n.sem("x_ln_loaded")
        stats_done = n.sem("stats_done")
        meanvar_done = n.sem("meanvar_done")
        var_done = n.sem("var_done")
        std_done = n.sem("std_done")
        rstd_step = n.sem("rstd_step")
        xn_done = n.sem("xn_done")
        xT_done = n.sem("xT_done")
        xT_high = n.sem("xT_high")
        xT_low = n.sem("xT_low")
        t_done = n.sem("t_done")
        t_high = n.sem("t_high")
        t_low = n.sem("t_low")
        score_done = n.sem("score_done")
        top_done = n.sem("top_done")
        chosen_done = n.sem("chosen_done")
        ranked_done = n.sem("ranked_done")
        leader_done = n.sem("leader_done")
        mask_done = n.sem("mask_done")
        h_done = n.sem("h_done")
        relu_done = n.sem("relu_done")
        mT_done = n.sem("mT_done")
        used_done = n.sem("used_done")
        used_high = n.sem("used_high")
        used_low = n.sem("used_low")
        out_done = n.sem("out_done")
        y_done = n.sem("y_done")
        raw_loaded = [n.sem(f"raw_loaded{i}") for i in range(2)]
        x_res_loaded = [n.sem(f"x_res_loaded{i}") for i in range(2)]
        y_stored = [n.sem(f"y_stored{i}") for i in range(2)]

        pieces = [(c1.rearrange("p c n -> p (c n)"), c1_s[:, 0].rearrange("p c n -> p (c n)"),
                   c1_s[:, 1].rearrange("p c n -> p (c n)"))]
        for f in range(FQ):
            at = slice(f * FN, (f + 1) * FN)
            pieces.append((c2[:, at], c2_s[:, at], None))
        for i in range(NI):
            pieces.append((w1[:, i].rearrange("p c n -> p (c n)"), w1_s[:, i, 0].rearrange("p c n -> p (c n)"),
                           w1_s[:, i, 1].rearrange("p c n -> p (c n)")))
        for i in range(NI):
            pieces.append((w2[i * P:(i + 1) * P], w2_s[:, i, 0], w2_s[:, i, 1]))
        C2, W1, W2 = 1, 1 + FQ, 1 + FQ + NI

        def tiles(engine, body):
            body(0, True, False)
            with engine.Fori(1, NT - 1) as T:
                body(T, False, False)
            body(NT - 1, False, True)

        block = stack.enter_context(nc.Block())

        @block.sync
        def _(sp):
            sp.dma_start(x_ln[:], x1_d[0]).then_inc(x_ln_loaded, 16)
            def next_tile(T):
                sp.wait_ge(xT_done, KC * (T + 1))
                sp.dma_start(x_ln[:], x1_d[T + 1]).then_inc(x_ln_loaded, 16)

            for i, (source, _, _) in enumerate(pieces):
                if i == W2:
                    next_tile(0)
                wait(sp, w_low, i - 1)
                sp.dma_start(raw[:, i % 2, 0:source.shape[1]], source).then_inc(raw_loaded[i % 2], 16)
            sp.wait_ge(w_low, len(pieces))

            def residual(T, c):
                if c < 2:
                    wait(sp, y_stored[c], 32 * T)
                else:
                    sp.wait_ge(y_stored[c % 2], 32 * T + 16)
                sp.dma_start(x_res[:, c % 2], x1_d[T, :, c]).then_inc(x_res_loaded[c % 2], 16)

            def store(T, c):
                sp.wait_ge(y_done, TC * T + c + 1)
                sp.dma_start(out[T, :, c], x_res[:, c % 2]).then_inc(y_stored[c % 2], 16)

            def body(T, first, last):
                if not first and not last:
                    next_tile(T)
                residual(T, 0)
                residual(T, 1)
                for c in range(TC):
                    store(T, c)
                    if c < 2:
                        residual(T, c + 2)

            tiles(sp, body)
            for i in range(2):
                sp.wait_ge(y_stored[i], 32 * NT)

        @block.gpsimd
        def _(pool):
            nc.gpsimd.memset(ident[:], 1.0).then_inc(ident_set, 1)
            pool.wait_ge(ident_set, 1)
            nc.gpsimd.affine_select(out=ident[:], in_=ident[:], compare_op=ALU.is_equal, fill=0.0, base=0,
                                    pattern=[[-1, P]], channel_multiplier=1).then_inc(ident_done, 1)
            nc.gpsimd.iota(rank[:], pattern=[[-1, SPARSE]], base=SPARSE, channel_multiplier=0,
                           allow_small_or_imprecise_dtypes=True).then_inc(rank_done, 1)

            def weight(i):
                source, high, low = pieces[i]
                pool.wait_ge(w_high, i + 1)
                if 1 <= i <= W1:
                    pool.wait_ge(w_low, i)
                cols = source.shape[1]
                if low is None:
                    nc.gpsimd.tensor_tensor(high[64:P], raw[64:P, i % 2, 0:cols], high[64:P],
                                            ALU.subtract).then_inc(w_low, 1)
                else:
                    nc.gpsimd.tensor_tensor(low, raw[:, i % 2, 0:cols], high, ALU.subtract).then_inc(w_low, 1)

            def body(T, first, last):
                for i in range(NI):
                    if first and i + 2 < NI:
                        weight(W2 + i + 2)
                    number = NI * T + i
                    pool.wait_ge(used_high, number + 1)
                    nc.gpsimd.tensor_tensor(used_s[:, i % 2, 1], hidden[:, i], used_s[:, i % 2, 0],
                                            ALU.subtract).then_inc(used_low, 1)

            for i in range(W2 + 2):
                weight(i)
            tiles(pool, body)

        @block.scalar
        def _(act):
            def weight(i):
                source, high, _ = pieces[i]
                act.wait_ge(raw_loaded[i % 2], 16 * (i // 2 + 1))
                nc.scalar.activation(high, raw[:, i % 2, 0:source.shape[1]], ACT.Copy).then_inc(w_high, 1)

            def root(T):
                act.wait_ge(var_done, T + 1)
                nc.scalar.activation(std[:], var[:], ACT.Sqrt).then_inc(std_done, 1)

            def split(T):
                for c in range(KC):
                    act.wait_ge(xT_done, KC * T + c + 1)
                    nc.scalar.activation(xT[:, 0, c], h_ps[c % 2][:], ACT.Copy).then_inc(xT_high, 1)
                act.wait_ge(t_done, T + 1)
                wait(act, score_done, TC * FQ * T)
                nc.scalar.activation(t_s[:], h_ps[0][:], ACT.Copy).then_inc(t_high, 1)

            def body(T, first, last):
                for i in range(NI):
                    number = NI * T + i
                    if first:
                        weight(W1 + i)
                    act.wait_ge(h_done, number + 1)
                    wait(act, used_low, number - NI + 1)
                    nc.scalar.activation(hidden[:, i], h_ps[i % 2][:], ACT.Relu).then_inc(relu_done, 1)
                if first:
                    weight(W2)
                    weight(W2 + 1)
                for i in range(NI):
                    number = NI * T + i
                    if first and i + 2 < NI:
                        weight(W2 + i + 2)
                    act.wait_ge(used_done, number + 1)
                    wait(act, out_done, number - 1)
                    nc.scalar.activation(used_s[:, i % 2, 0], hidden[:, i], ACT.Copy).then_inc(used_high, 1)
                    if i == 3 and not last:
                        root(T + 1)
                    if i == 9 and not last:
                        split(T + 1)

            for i in range(W1):
                weight(i)
            root(0)
            split(0)
            tiles(act, body)

        @block.vector
        def _(dve):
            def layer_norm(T):
                dve.wait_ge(x_ln_loaded, 16 * (T + 1))
                for c in range(TC):
                    last = nc.vector.bn_stats(stats[:, c], x_ln[:, c])
                last.then_inc(stats_done, 1)
                dve.wait_ge(stats_done, T + 1)
                wait(dve, xn_done, T)
                nc.vector.memset(spacer[:], 0.0)
                for c in range(TC):
                    last = nc.vector.bn_aggr(meanvar[:, c], stats[:, c])
                last.then_inc(meanvar_done, 1)
                dve.wait_ge(meanvar_done, T + 1)
                nc.vector.tensor_scalar(var[:], meanvar[:, :, 1], EPS, None, ALU.add).then_inc(var_done, 1)

            def normed(T):
                dve.wait_ge(std_done, T + 1)
                inverse_root(nc, dve, var, std, guess, step, rstd, rstd_step, 4 * T)
                for c in range(TC):
                    last = nc.vector.tensor_scalar(x_ln[:, c], x_ln[:, c], meanvar[:, c, 0:1], rstd[:, c:c + 1],
                                                   ALU.subtract, ALU.mult)
                last.then_inc(xn_done, 1)

            def split(T):
                for c in range(KC):
                    dve.wait_ge(xT_high, KC * T + c + 1)
                    nc.vector.tensor_tensor(xT[:, 1, c], h_ps[c % 2][:], xT[:, 0, c], ALU.subtract).then_inc(xT_low, 1)
                dve.wait_ge(t_high, T + 1)
                for start in (RANK_STEP, 3 * RANK_STEP):
                    rows = slice(start, start + RANK_STEP)
                    nc.vector.tensor_tensor(t_s[rows], h_ps[0][rows], t_s[rows], ALU.subtract).then_inc(t_low, 1)

            def choose(T, m):
                c, f = m // FQ, m % FQ
                number = TC * FQ * T + m
                scores = m_ps[m % 2][:, 0:FN].rearrange("p (b s) -> p b s", s=SPARSE)
                dve.wait_ge(score_done, number + 1)
                nc.vector.tensor_reduce(top[:, m % 2], scores, AXIS.X, ALU.max).then_inc(top_done, 1)
                dve.wait_ge(top_done, number + 1)
                if m == 0:
                    wait(dve, mT_done, NI * T)
                nc.vector.tensor_tensor(mask[:, c, f * FN:(f + 1) * FN].rearrange("p (b s) -> p b s", s=SPARSE), scores,
                                        top[:, m % 2].unsqueeze(2).to_broadcast([P, FB, SPARSE]),
                                        ALU.is_equal).then_inc(chosen_done, 1)
                if f == FQ - 1:
                    blocks = mask[:, c].rearrange("p (b s) -> p b s", s=SPARSE)
                    chunk = TC * T + c
                    dve.wait_ge(chosen_done, number + 1)
                    nc.vector.tensor_tensor(blocks, blocks,
                                            rank_bf[:].unsqueeze(1).to_broadcast([P, INTER // SPARSE, SPARSE]),
                                            ALU.mult).then_inc(ranked_done, 1)
                    dve.wait_ge(ranked_done, chunk + 1)
                    nc.vector.tensor_reduce(leader[:], blocks, AXIS.X, ALU.max).then_inc(leader_done, 1)
                    dve.wait_ge(leader_done, chunk + 1)
                    nc.vector.tensor_tensor(blocks, blocks,
                                            leader[:].unsqueeze(2).to_broadcast([P, INTER // SPARSE, SPARSE]),
                                            ALU.is_equal).then_inc(mask_done, 1)


            def body(T, first, last):
                for m in range(TC * FQ):
                    choose(T, m)
                for i in range(NI):
                    number = NI * T + i
                    dve.wait_ge(mT_done, number + 1)
                    dve.wait_ge(relu_done, number + 1)
                    nc.vector.tensor_tensor(hidden[:, i], hidden[:, i], m_ps[i % 2][:].bitcast(BF16)[:, 0:TT],
                                            ALU.mult).then_inc(used_done, 1)
                    if i == 2 and not last:
                        layer_norm(T + 1)
                    if i == 4 and not last:
                        normed(T + 1)
                    if i == 9 and not last:
                        split(T + 1)
                dve.wait_ge(out_done, NI * (T + 1))
                for c in range(TC):
                    dve.wait_ge(x_res_loaded[c % 2], 32 * T + 16 * (c // 2 + 1))
                    nc.vector.tensor_tensor(x_res[:, c % 2], x_res[:, c % 2], acc[c][:], ALU.add).then_inc(y_done, 1)

            dve.wait_ge(rank_done, 1)
            nc.vector.tensor_copy(rank_bf[:], rank[:]).then_inc(rank_bf_done, 1)
            dve.wait_ge(ident_done, 1)
            nc.vector.tensor_copy(ident_bf[:], ident[:]).then_inc(ident_bf_done, 1)
            dve.wait_ge(rank_bf_done, 1)
            layer_norm(0)
            normed(0)
            split(0)
            tiles(dve, body)

        @block.tensor
        def _(pe):
            def transpose(T):
                pe.wait_ge(xn_done, T + 1)
                for i in range(KC):
                    wait(pe, xT_low, KC * T + i - 1)
                    for c in range(TC):
                        last = nc.tensor.transpose(h_ps[i % 2][:, c * P:(c + 1) * P],
                                                   x_ln[:, c, i * P:(i + 1) * P], ident[:])
                    last.then_inc(xT_done, 1)
                pe.wait_ge(xT_low, KC * (T + 1))
                for i in range(KC):
                    last = three_passes(nc, h_ps[0][:], [c1_s[:, s, i] for s in range(2)],
                                        [xT[:, s, i] for s in range(2)], i == 0, i == KC - 1)
                last.then_inc(t_done, 1)

            def score(T, m):
                c, f = m // FQ, m % FQ
                number = TC * FQ * T + m
                wait(pe, chosen_done, number - 1)
                nc.tensor.matmul(m_ps[m % 2][:, 0:FN], t_s[:, c * P:(c + 1) * P], c2_s[:, f * FN:(f + 1) * FN],
                                 start=True, stop=True).then_inc(score_done, 1)

            def body(T, first, last):
                pe.wait_ge(t_low, 2 * (T + 1))
                wait(pe, used_done, NI * T)
                score(T, 0)
                score(T, 1)
                for i in range(NI):
                    number = NI * T + i
                    if first:
                        pe.wait_ge(w_low, W1 + i + 1)
                    wait(pe, relu_done, number - 1)
                    for c in range(KC):
                        last_mm = three_passes(nc, h_ps[i % 2][:], [w1_s[:, i, s, c] for s in range(2)],
                                               [xT[:, s, c] for s in range(2)], c == 0, c == KC - 1)
                    last_mm.then_inc(h_done, 1)
                    score(T, i + 2)
                for i in range(NI):
                    number = NI * T + i
                    if i == 0:
                        pe.wait_ge(mask_done, TC * (T + 1))
                        pe.wait_ge(chosen_done, TC * FQ * (T + 1))
                    wait(pe, used_done, number - 1)
                    for c in range(TC):
                        last_mm = nc.tensor.transpose(m_ps[i % 2][:].bitcast(BF16)[:, c * P:(c + 1) * P],
                                                      mask[:, c, i * P:(i + 1) * P], ident_bf[:])
                    last_mm.then_inc(mT_done, 1)
                    if i >= 1:
                        down(T, i - 1, first)
                    if i == 9 and not last:
                        transpose(T + 1)
                down(T, NI - 1, first)

            def down(T, i, first):
                number = NI * T + i
                pe.wait_ge(used_low, number + 1)
                if first:
                    pe.wait_ge(w_low, W2 + i + 1)
                if i == 0:
                    wait(pe, y_done, TC * T)
                for c in range(TC):
                    last_mm = three_passes(nc, acc[c][:], [used_s[:, i % 2, s, c * P:(c + 1) * P] for s in range(2)],
                                           [w2_s[:, i, s] for s in range(2)], i == 0, i == NI - 1)
                last_mm.then_inc(out_done, 1)

            pe.wait_ge(ident_done, 1)
            pe.wait_ge(ident_bf_done, 1)
            pe.wait_ge(w_low, W1)
            transpose(0)
            tiles(pe, body)


def build(nc, x, ctxT, wq, wk, wv, wo, c1, c2, w1, w2, out):
    kT_d = nc.dram_tensor("kT_d", [GROUPS, P, NKT, KT * KEYS], F32, kind="Internal").ap()
    v_d = nc.dram_tensor("v_d", [GROUPS, 2, P, NKT, KT, DH], F32, kind="Internal").ap()
    xnT_d = nc.dram_tensor("xnT_d", [2, NT, P, KC, 2, KT, L], F32, kind="Internal").ap()
    x1_d = nc.dram_tensor("x1_d", [NT, P, TC, D], F32, kind="Internal").ap()
    project_keys_values(nc, x, ctxT, wk, wv, kT_d, v_d, xnT_d)
    attend(nc, x, wq, wo, kT_d, v_d, xnT_d, x1_d)
    feed_forward(nc, x1_d, c1, c2, w1, w2, out)


def kernel(x, ctx_4096, L0_xattn_Wq, L0_xattn_Wk, L0_xattn_Wv, L0_xattn_Wo,
           L0_ffn_c1_w, L0_ffn_c2_w, L0_ffn_w1, L0_ffn_w2t):
    import numpy as np
    import concourse.bacc as bacc
    from concourse.bass_utils import run_bass_kernel_spmd

    x, ctx, wq, wk, wv, wo, c1, c2, w1, w2 = (np.asarray(a) for a in (
        x, ctx_4096, L0_xattn_Wq, L0_xattn_Wk, L0_xattn_Wv, L0_xattn_Wo,
        L0_ffn_c1_w, L0_ffn_c2_w, L0_ffn_w1, L0_ffn_w2t))
    c1_at = np.zeros((P, KC, P), c1.dtype)
    c2_at = np.zeros((P, INTER), c2.dtype)
    for r in range(P // RANK_STEP):
        at = slice(r * RANK_STEP, r * RANK_STEP + RANK)
        c1_at[:, :, at] = c1.reshape(RANK, KC, P).transpose(2, 1, 0)
        c2_at[at] = c2.T
    arrays = {
        "x": x.reshape(TOKENS, D),
        "ctxT": ctx.reshape(TOKENS, D).T,
        "wq": wq.reshape(KC, P, HEADS, DH).transpose(1, 2, 0, 3),
        "wk": wk, "wv": wv, "wo": wo,
        "c1": c1_at, "c2": c2_at,
        "w1": w1.reshape(NI, P, KC, P).transpose(3, 0, 2, 1),
        "w2": w2,
    }
    arrays = {name: np.ascontiguousarray(a) for name, a in arrays.items()}
    nc = bacc.Bacc("TRN2", target_bir_lowering=False, num_devices=1)
    aps = [nc.dram_tensor(name, list(a.shape), mybir.dt.from_np(a.dtype), kind="ExternalInput").ap()
           for name, a in arrays.items()]
    out = nc.dram_tensor("out", [TOKENS, D], F32, kind="ExternalOutput").ap()
    build(nc, *aps, out.rearrange("(t c p) d -> t p c d", c=TC, p=P))
    result = run_bass_kernel_spmd(nc, [arrays], core_ids=[0]).results[0]["out"]
    return result.reshape(B, L, D)
```

```python
from contextlib import ExitStack

import concourse.bass as bass
from concourse import mybir

F32 = mybir.dt.float32
F32R = mybir.dt.float32r
BF16 = mybir.dt.bfloat16
ALU = mybir.AluOpType
ACT = mybir.ActivationFunctionType
AXIS = mybir.AxisListType

P = 128
B, L, D = 32, 64, 512
HEADS, GROUPS, DH = 32, 4, 128
HG = HEADS // GROUPS
KEYS = 2 * L
KC = D // P
TOKENS = B * L
INTER, SPARSE = 1792, 32
NI = INTER // P
EPS = 1e-5

KT = 4
NKT = B // KT
TB = 8
TT = TB * L
NT = B // TB
TC = TT // P
FN = 448
FQ = INTER // FN
FB = FN // SPARSE
RANK = 16
RANK_STEP = 32


def wait(engine, semaphore, value):
    if isinstance(value, int) and value <= 0:
        return
    engine.wait_ge(semaphore, value)


class Names:

    def __init__(self, nc, stack, phase):
        self.nc, self.stack, self.phase = nc, stack, phase

    def sb(self, name, shape, dtype=F32):
        return self.stack.enter_context(self.nc.sbuf_tensor(f"{self.phase}_{name}", shape, dtype))

    def ps(self, name, shape=(P, 512), dtype=F32):
        return self.stack.enter_context(self.nc.psum_tensor(f"{self.phase}_{name}", list(shape), dtype))

    def sem(self, name):
        return self.stack.enter_context(self.nc.semaphore(f"{self.phase}_{name}"))


def three_passes(nc, out, stationary, moving, start, stop):
    (sh, sl), (mh, ml) = stationary, moving
    nc.tensor.matmul(out, sh, mh, start=start, stop=False)
    nc.tensor.matmul(out, sh, ml, start=False, stop=False)
    return nc.tensor.matmul(out, sl, mh, start=False, stop=stop)


def inverse_root(nc, dve, var, std, guess, step, out, done, before):
    nc.vector.reciprocal(guess[:], std[:]).then_inc(done, 1)
    dve.wait_ge(done, before + 1)
    nc.vector.tensor_tensor(step[:, 0], guess[:], guess[:], ALU.mult).then_inc(done, 1)
    dve.wait_ge(done, before + 2)
    nc.vector.scalar_tensor_tensor(step[:, 1], var[:], -0.5, step[:, 0], ALU.mult, ALU.mult).then_inc(done, 1)
    dve.wait_ge(done, before + 3)
    nc.vector.scalar_tensor_tensor(out[:], step[:, 1], 1.5, guess[:], ALU.add, ALU.mult).then_inc(done, 1)
    dve.wait_ge(done, before + 4)


def set_identity(nc, pool, ident, ident_set, ident_done):
    nc.gpsimd.memset(ident[:], 1.0).then_inc(ident_set, 1)
    pool.wait_ge(ident_set, 1)
    nc.gpsimd.affine_select(out=ident[:], in_=ident[:], compare_op=ALU.is_equal, fill=0.0, base=0,
                            pattern=[[-1, P]], channel_multiplier=1).then_inc(ident_done, 1)


class Shared:

    RAW = 4
    W1_EARLY = 3

    def __init__(self, nc, stack):
        n = Names(nc, stack, "sh")
        self.ident = n.sb("ident", [P, P])
        self.xT = [n.sb(f"xT{i}", [P, 2, KC, TT], F32R) for i in range(2)]
        self.wq_s = n.sb("wq_s", [P, 2, 2, KC, DH], F32R)
        self.t_s = n.sb("t_s", [P, TT], F32R)
        self.ident_set = n.sem("ident_set")
        self.ident_done = n.sem("ident_done")
        self.k_stored = [n.sem(f"k_stored{i}") for i in range(2)]
        self.v_stored = [n.sem(f"v_stored{i}") for i in range(2)]
        self.x1_stored = n.sem("x1_stored")
        self.xT_loaded = [n.sem(f"xT_loaded{i}") for i in range(2)]
        self.wq_loaded = [n.sem(f"wq_loaded{i}") for i in range(self.RAW)]
        self.wq_high = n.sem("wq_high")
        self.wq_low = n.sem("wq_low")
        self.c1_loaded = n.sem("c1_loaded")
        self.c2_loaded = n.sem("c2_loaded")
        self.w1_loaded = n.sem("w1_loaded")
        self.c1_high = n.sem("c1_high")
        self.c1_low = n.sem("c1_low")
        self.c2_high = n.sem("c2_high")
        self.c2_low = n.sem("c2_low")
        self.w1_high = n.sem("w1_high")
        self.w1_low = n.sem("w1_low")
        assert self.W1_EARLY + 1 == TT // P
        later = self.xT[1][:].rearrange("p s c n -> p (s c n)").rearrange(
            "p (i s c n) -> p i s c n", i=self.W1_EARLY + 1, s=2, c=KC)
        self.w1_s = later[:, :self.W1_EARLY]
        self.c1_s = later[:, self.W1_EARLY]
        self.c2_s = self.wq_s[:].rearrange("p i s c n -> p (i s c n)")[:, :INTER]

    def load_xT(self, sp, xnT_d, T, half):
        for part in range(2):
            sp.dma_start(self.xT[half][:, part].bitcast(F32).rearrange("p c n -> p (c n)"),
                         xnT_d[part, T].rearrange("p c i n t -> p (c i n t)")).then_inc(self.xT_loaded[half], 16)

    def load_wq(self, sp, wq, wq_raw, head):
        at = head % self.RAW
        sp.dma_start(wq_raw[:, at], wq[:, head]).then_inc(self.wq_loaded[at], 16)


class Front:

    def __init__(self, nc, stack, shared, x1_d):
        n = Names(nc, stack, "fr")
        self.nc, self.shared, self.x1_d = nc, shared, x1_d
        self.xT, self.t_s = shared.xT[0], shared.t_s
        self.x = n.sb("x", [P, TC, D])
        self.stats = n.sb("stats", [P, TC, 6])
        self.meanvar = n.sb("meanvar", [P, TC, 2])
        self.var = n.sb("var", [P, TC])
        self.std = n.sb("std", [P, TC])
        self.guess = n.sb("guess", [P, TC])
        self.step = n.sb("step", [P, 2, TC])
        self.rstd = n.sb("rstd", [P, TC])
        self.spacer = n.sb("spacer", [P, 1])
        self.loaded = n.sem("loaded")
        self.stats_done = n.sem("stats_done")
        self.meanvar_done = n.sem("meanvar_done")
        self.var_done = n.sem("var_done")
        self.std_done = n.sem("std_done")
        self.rstd_step = n.sem("rstd_step")
        self.norm_done = n.sem("norm_done")
        self.xT_done = n.sem("xT_done")
        self.xT_high = n.sem("xT_high")
        self.xT_low = n.sem("xT_low")
        self.t_done = n.sem("t_done")
        self.t_high = n.sem("t_high")
        self.t_low = n.sem("t_low")

    def load(self, sp, T):
        sp.dma_start(self.x[:], self.x1_d[T]).then_inc(self.loaded, 16)

    def statistics(self, dve, T, c):
        if c == 0:
            dve.wait_ge(self.loaded, 16 * (T + 1))
        self.nc.vector.bn_stats(self.stats[:, c], self.x[:, c]).then_inc(self.stats_done, 1)

    def variance(self, dve, T):
        nc = self.nc
        dve.wait_ge(self.stats_done, TC * (T + 1))
        wait(dve, self.norm_done, TC * T)
        nc.vector.memset(self.spacer[:], 0.0)
        for c in range(TC):
            last = nc.vector.bn_aggr(self.meanvar[:, c], self.stats[:, c])
        last.then_inc(self.meanvar_done, 1)
        dve.wait_ge(self.meanvar_done, T + 1)
        nc.vector.tensor_scalar(self.var[:], self.meanvar[:, :, 1], EPS, None, ALU.add).then_inc(self.var_done, 1)

    def root(self, act, T):
        act.wait_ge(self.var_done, T + 1)
        self.nc.scalar.activation(self.std[:], self.var[:], ACT.Sqrt).then_inc(self.std_done, 1)

    def invert(self, dve, T):
        dve.wait_ge(self.std_done, T + 1)
        inverse_root(self.nc, dve, self.var, self.std, self.guess, self.step, self.rstd, self.rstd_step, 4 * T)

    def apply(self, dve, T, c):
        self.nc.vector.tensor_scalar(self.x[:, c], self.x[:, c], self.meanvar[:, c, 0:1], self.rstd[:, c:c + 1],
                                     ALU.subtract, ALU.mult).then_inc(self.norm_done, 1)

    def transpose(self, pe, T, c, banks):
        pe.wait_ge(self.norm_done, TC * (T + 1))
        wait(pe, self.xT_low, KC * T + c - 1)
        for i in range(TC):
            last = self.nc.tensor.transpose(banks[c % 2][:, i * P:(i + 1) * P], self.x[:, i, c * P:(c + 1) * P],
                                            self.shared.ident[:])
        last.then_inc(self.xT_done, 1)

    def high_xT(self, act, T, c, banks):
        act.wait_ge(self.xT_done, KC * T + c + 1)
        self.nc.scalar.activation(self.xT[:, 0, c], banks[c % 2][:], ACT.Copy).then_inc(self.xT_high, 1)

    def low_xT(self, dve, T, c, banks):
        dve.wait_ge(self.xT_high, KC * T + c + 1)
        self.nc.vector.tensor_tensor(self.xT[:, 1, c], banks[c % 2][:], self.xT[:, 0, c],
                                     ALU.subtract).then_inc(self.xT_low, 1)

    def project_t(self, pe, T, banks):
        pe.wait_ge(self.xT_low, KC * (T + 1))
        for c in range(KC):
            last = three_passes(self.nc, banks[0][:], [self.shared.c1_s[:, s, c] for s in range(2)],
                                [self.xT[:, s, c] for s in range(2)], c == 0, c == KC - 1)
        last.then_inc(self.t_done, 1)

    def high_t(self, act, T, banks):
        act.wait_ge(self.t_done, T + 1)
        self.nc.scalar.activation(self.t_s[:], banks[0][:], ACT.Copy).then_inc(self.t_high, 1)

    def low_t(self, dve, T, banks):
        dve.wait_ge(self.t_high, T + 1)
        for start in (RANK_STEP, 3 * RANK_STEP):
            rows = slice(start, start + RANK_STEP)
            self.nc.vector.tensor_tensor(self.t_s[rows], banks[0][rows], self.t_s[rows],
                                         ALU.subtract).then_inc(self.t_low, 1)


def high_wq(nc, act, shared, wq_raw, head):
    act.wait_ge(shared.wq_loaded[head], 16)
    nc.scalar.activation(shared.wq_s[:, head, 0], wq_raw[:, head], ACT.Copy).then_inc(shared.wq_high, 1)


def low_wq(nc, pool, shared, wq_raw, head):
    pool.wait_ge(shared.wq_high, head + 1)
    nc.gpsimd.tensor_tensor(shared.wq_s[:, head, 1], wq_raw[:, head], shared.wq_s[:, head, 0],
                            ALU.subtract).then_inc(shared.wq_low, 1)


def project_keys_values(nc, shared, wq_raw, x, ctxT, wq, wk, wv, kT_d, v_d, xnT_d):
    with ExitStack() as stack:
        n = Names(nc, stack, "kv")
        ident, ident_done = shared.ident, shared.ident_done
        k_stored, v_stored = shared.k_stored, shared.v_stored
        h = n.sb("h", [P, 2, 2, KC, KT, KEYS], F32R)
        k_out = n.sb("k_out", [P, 2, GROUPS, KT * KEYS])
        v_out = n.sb("v_out", [P, 2, 2, GROUPS, KT, DH], F32R)
        w_raw = n.sb("w_raw", [P, 2, KC, D])
        w = n.sb("w", [P, 2, 2, KC, D], F32R)
        x_in = n.sb("x_in", [P, 2, 2, D])
        c_in = n.sb("c_in", [P, 2, KC, KT * L])
        xn = n.sb("xn", [P, 2, D])
        stats = n.sb("stats", [P, 2, 6])
        meanvar = n.sb("meanvar", [P, 2, 2])
        std = n.sb("std", [P, 2])
        var = n.sb("var", [P, 2])
        guess = n.sb("guess", [P, 2])
        step = n.sb("step", [P, 2, 2])
        rstd = n.sb("rstd", [P, 2])
        spacer = n.sb("spacer", [P, 1])
        xT = [n.ps(f"xT{i}", (P, 2, KT * L)) for i in range(2)]
        proj = [n.ps(f"proj{i}") for i in range(4)]

        w_in = [n.sem(f"w_in{i}") for i in range(4)]
        w_high = n.sem("w_high")
        w_low = n.sem("w_low")
        x_loaded = [n.sem(f"x_loaded{i}") for i in range(2)]
        c_loaded = [n.sem(f"c_loaded{i}") for i in range(2)]
        stats_done = n.sem("stats_done")
        meanvar_done = n.sem("meanvar_done")
        std_done = n.sem("std_done")
        var_done = n.sem("var_done")
        rstd_step = n.sem("rstd_step")
        xn_done = n.sem("xn_done")
        xT_done = n.sem("xT_done")
        xT_high = n.sem("xT_high")
        xT_low = n.sem("xT_low")
        c_high = n.sem("c_high")
        c_low = n.sem("c_low")
        k_done = n.sem("k_done")
        v_done = n.sem("v_done")
        k_copied = n.sem("k_copied")
        v_high = n.sem("v_high")
        v_low = n.sem("v_low")
        x_stored = [n.sem(f"x_stored{i}") for i in range(2)]

        x_rows = x.rearrange("(i r p) d -> i p r d", r=2, p=P)
        c_cols = ctxT.rearrange("(c p) (i n) -> i p c n", p=P, i=NKT)

        def tiles(engine, body):
            for p in range(2):
                body(0, p)
            with engine.Fori(1, NKT // 2 - 1) as pair:
                for p in range(2):
                    body(pair, p)
            for p in range(2):
                body(NKT // 2 - 1, p)

        def following(pair, p):
            if p == 0:
                return pair, 1
            return None if isinstance(pair, int) and pair == NKT // 2 - 1 else (pair + 1, 0)

        block = stack.enter_context(nc.Block())

        @block.sync
        def _(sp):
            def load_x(pair, p):
                i = 2 * pair + p
                wait(sp, xn_done, i - 1)
                sp.dma_start(x_in[:, p], x_rows[i]).then_inc(x_loaded[p], 16)

            def load_c(pair, p):
                i = 2 * pair + p
                wait(sp, c_low, i - 1)
                sp.dma_start(c_in[:, p], c_cols[i]).then_inc(c_loaded[p], 16)

            load_x(0, 0)
            for s, src in enumerate((wk, wv)):
                for half in range(2):
                    at = slice(half * KC // 2, (half + 1) * KC // 2)
                    sp.dma_start(w_raw[:, s, at],
                                 src.rearrange("(c p) n -> p c n", p=P)[:, at]).then_inc(w_in[2 * s + half], 16)
                if s == 0:
                    load_c(0, 0)
            load_x(0, 1)
            load_c(0, 1)

            def body(pair, p):
                i = 2 * pair + p
                if not (isinstance(pair, int) and pair == NKT // 2 - 1):
                    load_x(pair + 1, p)
                    load_c(pair + 1, p)
                elif p == 0:
                    for q in range(2):
                        sp.wait_ge(x_stored[q], 32 * pair)
                    shared.load_xT(sp, xnT_d, 0, 0)
                    for head in range(shared.RAW):
                        shared.load_wq(sp, wq, wq_raw, head)
                for part in range(2):
                    wait(sp, xT_low, 2 * i + 2)
                    sp.dma_start(xnT_d[part, pair, :, :, p],
                                 h[:, p, part, :, :, L:].bitcast(F32)).then_inc(x_stored[p], 16)
                wait(sp, k_copied, GROUPS * (i + 1))
                sp.dma_start(kT_d[:, :, i].rearrange("g p n -> p g n"), k_out[:, p]).then_inc(k_stored[p], 16)
                wait(sp, v_low, KT * (i + 1))
                for part in range(2):
                    sp.dma_start(v_d[:, part, :, i].rearrange("g p n d -> p g (n d)"),
                                 v_out[:, p, part].rearrange("p g n d -> p g (n d)").bitcast(F32)).then_inc(v_stored[p], 16)

            tiles(sp, body)
            for p in range(2):
                sp.wait_ge(x_stored[p], 16 * NKT)

        @block.gpsimd
        def _(pool):
            set_identity(nc, pool, ident, shared.ident_set, ident_done)

            def split(pair, p):
                i = 2 * pair + p
                pool.wait_ge(c_high, i + 1)
                for c in range(2):
                    last = nc.gpsimd.tensor_tensor(h[:, p, 1, 2 * c:2 * c + 2, :, 0:L],
                                                   c_in[:, p, 2 * c:2 * c + 2].rearrange("p c (n t) -> p c n t", n=KT),
                                                   h[:, p, 0, 2 * c:2 * c + 2, :, 0:L], ALU.subtract)
                last.then_inc(c_low, 1)

            def body(pair, p):
                after = following(pair, p)
                if after:
                    split(*after)

            split(0, 0)
            tiles(pool, body)
            for head in range(2):
                low_wq(nc, pool, shared, wq_raw, head)

        @block.scalar
        def _(act):
            def root(pair, p):
                act.wait_ge(var_done, 2 * pair + p + 1)
                nc.scalar.activation(std[:], var[:], ACT.Sqrt).then_inc(std_done, 1)

            def context(pair, p):
                i = 2 * pair + p
                act.wait_ge(c_loaded[p], 16 * (pair + 1))
                wait(act, v_done, KT * (i - 1))
                wait(act, x_stored[p], 32 * pair)
                nc.scalar.activation(h[:, p, 0, :, :, 0:L],
                                     c_in[:, p].rearrange("p c (n t) -> p c n t", n=KT), ACT.Copy).then_inc(c_high, 1)

            def split(pair, p):
                i = 2 * pair + p
                act.wait_ge(xT_done, i + 1)
                for c in range(2):
                    nc.scalar.activation(h[:, p, 0, 2 * c:2 * c + 2, :, L:],
                                         xT[c][:].rearrange("p c (n t) -> p c n t", n=KT), ACT.Copy).then_inc(xT_high, 1)

            def body(pair, p):
                i = 2 * pair + p
                after = following(pair, p)
                if after:
                    root(*after)
                    context(*after)
                else:
                    for head in range(2):
                        high_wq(nc, act, shared, wq_raw, head)
                wait(act, k_stored[p], 16 * pair)
                for g in range(GROUPS):
                    act.wait_ge(k_done, GROUPS * i + g + 1)
                    nc.scalar.activation(k_out[:, p, g], proj[g][:], ACT.Copy).then_inc(k_copied, 1)
                if after:
                    split(*after)
                wait(act, v_stored[p], 32 * pair)
                for b in range(KT):
                    act.wait_ge(v_done, KT * i + b + 1)
                    nc.scalar.activation(v_out[:, p, 0, :, b], proj[b][:].rearrange("p (g d) -> p g d", g=GROUPS),
                                         ACT.Copy).then_inc(v_high, 1)

            root(0, 0)
            for s in range(2):
                for half in range(2):
                    act.wait_ge(w_in[2 * s + half], 16)
                    at = slice(half * KC // 2, (half + 1) * KC // 2)
                    nc.scalar.activation(w[:, s, 0, at], w_raw[:, s, at], ACT.Copy).then_inc(w_high, 1)
                if s == 0:
                    context(0, 0)
                    split(0, 0)
            tiles(act, body)

        @block.vector
        def _(dve):
            def layer_norm(pair, p):
                i = 2 * pair + p
                dve.wait_ge(x_loaded[p], 16 * (pair + 1))
                for r in range(2):
                    last = nc.vector.bn_stats(stats[:, r], x_in[:, p, r])
                last.then_inc(stats_done, 1)
                dve.wait_ge(stats_done, i + 1)
                wait(dve, std_done, i)
                nc.vector.memset(spacer[:], 0.0)
                for r in range(2):
                    last = nc.vector.bn_aggr(meanvar[:, r], stats[:, r])
                last.then_inc(meanvar_done, 1)
                dve.wait_ge(meanvar_done, i + 1)
                nc.vector.tensor_scalar(var[:], meanvar[:, :, 1], EPS, None, ALU.add).then_inc(var_done, 1)
                dve.wait_ge(std_done, i + 1)
                inverse_root(nc, dve, var, std, guess, step, rstd, rstd_step, 4 * i)
                wait(dve, xT_done, i)
                for r in range(2):
                    last = nc.vector.tensor_scalar(xn[:, r], x_in[:, p, r], meanvar[:, r, 0:1], rstd[:, r:r + 1],
                                                   ALU.subtract, ALU.mult)
                last.then_inc(xn_done, 1)

            def split(pair, p):
                i = 2 * pair + p
                for c in range(2):
                    dve.wait_ge(xT_high, 2 * i + c + 1)
                    nc.vector.tensor_tensor(h[:, p, 1, 2 * c:2 * c + 2, :, L:],
                                            xT[c][:].rearrange("p c (n t) -> p c n t", n=KT),
                                            h[:, p, 0, 2 * c:2 * c + 2, :, L:], ALU.subtract).then_inc(xT_low, 1)

            def body(pair, p):
                i = 2 * pair + p
                after = following(pair, p)
                if after:
                    layer_norm(*after)
                    split(*after)
                for b in range(KT):
                    dve.wait_ge(v_high, KT * i + b + 1)
                    nc.vector.tensor_tensor(v_out[:, p, 1, :, b], proj[b][:].rearrange("p (g d) -> p g d", g=GROUPS),
                                            v_out[:, p, 0, :, b], ALU.subtract).then_inc(v_low, 1)

            layer_norm(0, 0)
            for s in range(2):
                for half in range(2):
                    at = slice(half * KC // 2, (half + 1) * KC // 2)
                    dve.wait_ge(w_high, 2 * s + half + 1)
                    nc.vector.tensor_tensor(w[:, s, 1, at], w_raw[:, s, at], w[:, s, 0, at],
                                            ALU.subtract).then_inc(w_low, 1)
                if s == 0:
                    split(0, 0)
            tiles(dve, body)

        @block.tensor
        def _(pe):
            def transpose(pair, p):
                i = 2 * pair + p
                pe.wait_ge(xn_done, i + 1)
                wait(pe, xT_low, 2 * i)
                for c in range(KC):
                    for r in range(2):
                        last = nc.tensor.transpose(xT[c // 2][:, c % 2, r * P:(r + 1) * P],
                                                   xn[:, r, c * P:(c + 1) * P], ident[:])
                last.then_inc(xT_done, 1)

            def body(pair, p):
                i = 2 * pair + p
                pe.wait_ge(xT_low, 2 * i + 2)
                pe.wait_ge(c_low, i + 1)
                for g in range(GROUPS):
                    wait(pe, v_low, KT * (i - 1) + g + 1)
                    for c in range(KC):
                        last = three_passes(nc, proj[g][:],
                                            [w[:, 0, s, c, g * DH:(g + 1) * DH] for s in range(2)],
                                            [h[:, p, s, c].rearrange("p n t -> p (n t)") for s in range(2)],
                                            c == 0, c == KC - 1)
                    last.then_inc(k_done, 1)
                after = following(pair, p)
                if after:
                    transpose(*after)
                pe.wait_ge(w_low, 4)
                for b in range(KT):
                    pe.wait_ge(k_copied, GROUPS * i + b + 1)
                    for c in range(KC):
                        last = three_passes(nc, proj[b][:], [h[:, p, s, c, b] for s in range(2)],
                                            [w[:, 1, s, c] for s in range(2)], c == 0, c == KC - 1)
                    last.then_inc(v_done, 1)

            pe.wait_ge(ident_done, 1)
            transpose(0, 0)
            pe.wait_ge(w_low, 2)
            tiles(pe, body)


def attend(nc, shared, wq_raw, front, x, wq, wo, c1, c2, w1, kT_d, v_d, xnT_d, x1_d):
    with ExitStack() as stack:
        n = Names(nc, stack, "at")
        RAW, ident, xT, wq_s = shared.RAW, shared.ident, shared.xT, shared.wq_s
        xT_loaded, wq_loaded, wq_high, wq_low = shared.xT_loaded, shared.wq_loaded, shared.wq_high, shared.wq_low
        HALVES = 2
        ROOT_AT, XT_AT, T_AT = 0, 3, 7
        q = n.sb("q", [P, 2, TB, HG, L])
        x1 = n.sb("x1", [P, TC, D])
        v = n.sb("v", [P, 2, 2, TB, DH], F32R)
        o = n.sb("o", [P, 2, 2, HG, TT], F32R)
        wo_raw = n.sb("wo_raw", [P, 2, D])
        wo_s = n.sb("wo_s", [P, 2, 2, D], F32R)
        k = n.sb("k", [P, 2, TB, KEYS])
        negmax = n.sb("negmax", [P, 4])
        total = n.sb("total", [P, 4])
        inverse = n.sb("inverse", [P, 4])
        e = n.sb("e", [P, 4, KEYS])
        prob = n.sb("prob", [P, 4, KEYS])
        probT = n.sb("probT", [P, 2, 512], F32R)
        q_ps = n.ps("q_ps")
        s_ps = n.ps("s_ps", (P, 4, KEYS))
        pT_ps = n.ps("pT_ps")
        o_ps = n.ps("o_ps")
        acc = [n.ps(f"acc{c}") for c in range(TC)]
        front_banks = [q_ps, pT_ps]
        c2_raw = q[:, 0].rearrange("p n h t -> p (n h t)")[:, :INTER]

        wo_loaded = [n.sem(f"wo_loaded{i}") for i in range(2)]
        k_loaded = [n.sem(f"k_loaded{i}") for i in range(2)]
        v_loaded = [n.sem(f"v_loaded{i}") for i in range(2)]
        x_loaded = n.sem("x_loaded")
        x1_stored = shared.x1_stored
        wo_high = n.sem("wo_high")
        wo_low = n.sem("wo_low")
        q_done = n.sem("q_done")
        q_copied = n.sem("q_copied")
        s_done = n.sem("s_done")
        max_done = n.sem("max_done")
        e_done = n.sem("e_done")
        inverse_done = n.sem("inverse_done")
        prob_done = n.sem("prob_done")
        pT_done = n.sem("pT_done")
        pT_high = n.sem("pT_high")
        pT_low = n.sem("pT_low")
        pv_done = n.sem("pv_done")
        o_high = n.sem("o_high")
        o_low = n.sem("o_low")
        wo_done = n.sem("wo_done")
        acc_done = n.sem("acc_done")
        acc_read = n.sem("acc_read")

        x_rows = x.rearrange("(t c p) d -> t p c d", c=TC, p=P)

        def rounds(engine, body):
            for g in range(GROUPS):
                body(0, g, True, g >= 1, g >= 2)
            with engine.Fori(1, NT) as T:
                for g in range(GROUPS):
                    body(T, g, True, True, True)
            body(NT, 0, False, True, True)
            body(NT, 1, False, False, True)

        def q_bank(T, g, j):
            return acc[0] if alternating(T, g) and j % 2 else q_ps

        def alternating(T, g):
            return isinstance(T, int) and T == 0 and g < 2

        def earlier(T, g, steps):
            return (T, g - steps) if g >= steps else (T - 1, g - steps + GROUPS)

        def drain_slots(T, g, j):
            return [j if isinstance(T, int) and (T, g) == (NT, drain) else None for drain in range(2)]

        def next_wo(T, g, j, c):
            first = isinstance(T, int) and (T, g, j) == (0, 1, HG - 1)
            last = isinstance(T, int) and (T, g, j) == (NT, 1, HG - 1)
            if last or not (c or first):
                return None
            number = HG * (GROUPS * T + g - 2) + j + 1
            head_group = (g - 2) % GROUPS if j < HG - 1 else (g - 1) % GROUPS
            return number, head_group, (j + 1) % HG


        block = stack.enter_context(nc.Block())

        @block.sync
        def _(sp):
            def body(T, g, a, b, c):
                u = GROUPS * T + g
                if isinstance(T, int) and (T, g) == (NT, 0):
                    sp.wait_ge(x1_stored, 16)
                    front.load(sp, 0)
                    sp.wait_ge(wq_low, HG * GROUPS * NT)
                    sp.dma_start(wq_raw[:, 0], c1).then_inc(shared.c1_loaded, 16)
                    sp.dma_start(wq_raw[:, 1:], w1[:, :shared.W1_EARLY]).then_inc(shared.w1_loaded, 16)
                    sp.wait_ge(s_done, TB * (GROUPS * NT - 1))
                    sp.dma_start(c2_raw, c2).then_inc(shared.c2_loaded, 16)
                for j in range(HG):
                    slot = HG * u + j
                    first = isinstance(T, int) and T == 0
                    if a and j == 0 and g == 0 and not first:
                        load_xT(T, 0)
                    if a and not (first and slot < RAW):
                        wait(sp, wq_low, slot - RAW + 1)
                        shared.load_wq(sp, wq, wq_raw, HG * g + j)
                    after = next_wo(T, g, j, c)
                    if after:
                        number, wg, head = after
                        wait(sp, wo_low, number - 1)
                        row = (HG * wg + head) * DH
                        sp.dma_start(wo_raw[:, head % 2], wo[row:row + DH]).then_inc(wo_loaded[head % 2], 16)
                    if a and j == 4:
                        wait(sp, pv_done, TB * (u - 1))
                        if isinstance(u, int) and u == 0:
                            for p in range(2):
                                sp.wait_ge(shared.k_stored[p], 16 * NKT // 2)
                                sp.wait_ge(shared.v_stored[p], 16 * NKT)
                        sp.dma_start(k[:, g % 2].rearrange("p (i n) t -> p i (n t)", i=2),
                                     kT_d[g, :, bass.ds(2 * T, 2)]).then_inc(k_loaded[g % 2], 16)
                        for part in range(2):
                            sp.dma_start(v[:, g % 2, part].bitcast(F32).rearrange("p (i n) d -> p i (n d)", i=2),
                                         v_d[g, part, :, bass.ds(2 * T, 2)].rearrange("p i n d -> p i (n d)")
                                         ).then_inc(v_loaded[g % 2], 16)
                    if a and j == 7 and g == 0:
                        load_xT(T, 1)
                    if a and j == 6 and g == 2:
                        wait(sp, x1_stored, 16 * T)
                        sp.dma_start(x1[:], x_rows[T]).then_inc(x_loaded, 16)

            def load_xT(T, half):
                u = GROUPS * T + 2 * half
                wait(sp, q_done, HG * (u - 2))
                shared.load_xT(sp, xnT_d, T, half)

            rounds(sp, body)

        @block.gpsimd
        def _(pool):
            def body(T, g, a, b, c):
                u = GROUPS * T + g
                for j in range(HG):
                    if a and not (isinstance(T, int) and u == 0 and j < 2):
                        pool.wait_ge(wq_high, HG * u + j + 1)
                        nc.gpsimd.tensor_tensor(wq_s[:, j % 2, 1], wq_raw[:, j % RAW], wq_s[:, j % 2, 0],
                                                ALU.subtract).then_inc(wq_low, 1)
                    after = next_wo(T, g, j, c)
                    if after:
                        number, _, head = after
                        pool.wait_ge(wo_high, number + 1)
                        nc.gpsimd.tensor_tensor(wo_s[:, head % 2, 1], wo_raw[:, head % 2], wo_s[:, head % 2, 0],
                                                ALU.subtract).then_inc(wo_low, 1)
                    drain0, _ = drain_slots(T, g, j)
                    if drain0 == 0:
                        pool.wait_ge(shared.c1_high, 1)
                        nc.gpsimd.tensor_tensor(shared.c1_s[:, 1], wq_raw[:, 0], shared.c1_s[:, 0],
                                                ALU.subtract).then_inc(shared.c1_low, 1)
                    if drain0 in range(1, 1 + shared.W1_EARLY):
                        pool.wait_ge(shared.w1_high, drain0)
                        nc.gpsimd.tensor_tensor(shared.w1_s[:, drain0 - 1, 1], wq_raw[:, drain0],
                                                shared.w1_s[:, drain0 - 1, 0], ALU.subtract).then_inc(shared.w1_low, 1)

            rounds(pool, body)

        @block.scalar
        def _(act):
            def high_wq(T, g, j):
                u = GROUPS * T + g
                act.wait_ge(wq_loaded[j % RAW], 16 * (2 * u + j // RAW + 1))
                wait(act, q_done, HG * u + j - 1)
                nc.scalar.activation(wq_s[:, j % 2, 0], wq_raw[:, j % RAW], ACT.Copy).then_inc(wq_high, 1)

            def copy_q(T, g, j):
                u = GROUPS * T + g
                act.wait_ge(q_done, HG * u + j + 1)
                if j == 0:
                    wait(act, s_done, TB * (u - 1))
                nc.scalar.activation(q[:, g % 2, :, j], q_bank(T, g, j)[:].rearrange("p (n t) -> p n t", n=TB),
                                     ACT.Copy, scale=DH ** -0.5).then_inc(q_copied, 1)

            def high_o(T, g, j, b, c):
                if not (b if j else c):
                    return
                u = GROUPS * T + g
                og, oj = (earlier(T, g, 1)[1], j - 1) if j else (earlier(T, g, 2)[1], HG - 1)
                act.wait_ge(pv_done, HG * (u - 1) + j)
                if oj == 0:
                    wait(act, wo_done, HG * (u - 2))
                nc.scalar.activation(o[:, og % 2, 0, :, oj * L:(oj + 1) * L],
                                     o_ps[:].rearrange("p (h t) -> p h t", h=HG), ACT.Copy).then_inc(o_high, 1)

            def body(T, g, a, b, c):
                u = GROUPS * T + g
                steady = a and b and c
                late = a and b and not c
                for j in range(HG):
                    slot = HG * u + j
                    batch = slot - HG
                    if steady:
                        high_o(T, g, j, b, c)
                    filling = isinstance(T, int) and 0 < slot < 2 * HG
                    if a and not (isinstance(T, int) and slot <= 2 * HG):
                        high_wq(T, g, j)
                    if filling and b:
                        high_wq(0, (g * HG + j + 1) // HG, (j + 1) % HG)
                    if b:
                        act.wait_ge(max_done, batch + 1)
                        wait(act, prob_done, HALVES * batch)
                        for i in range(4):
                            last = nc.scalar.activation(e[:, i], s_ps[:, i], ACT.Exp, bias=negmax[:, i:i + 1],
                                                        accum_out=total[:, i:i + 1])
                            if i % 2:
                                last.then_inc(e_done, 1)
                    if not steady:
                        high_o(T, g, j, b, c)
                    if late and j >= 1:
                        copy_q(T, g, j - 1)
                    if b:
                        act.wait_ge(pT_done, batch + 1)
                        wait(act, pv_done, batch)
                        nc.scalar.activation(probT[:, 0], pT_ps[:], ACT.Copy).then_inc(pT_high, 1)
                    if filling and not b:
                        high_wq(0, (g * HG + j + 1) // HG, (j + 1) % HG)
                    after = next_wo(T, g, j, c)
                    if after:
                        number, _, head = after
                        act.wait_ge(wo_loaded[head % 2], 16 * (number // 2 + 1) if isinstance(number, int)
                                    else 16 * (4 * (u - 2) + (j + 1) // 2 + 1))
                        wait(act, wo_done, number - 1)
                        nc.scalar.activation(wo_s[:, head % 2, 0], wo_raw[:, head % 2], ACT.Copy).then_inc(wo_high, 1)
                    if a and (not late or j == HG - 1):
                        copy_q(T, g, j)
                    if c and g == 2 and j == 1 and not (isinstance(T, int) and T == 0):
                        store_x1(T)
                    drain0, drain1 = drain_slots(T, g, j)
                    if drain0 == 0:
                        act.wait_ge(shared.c1_loaded, 16)
                        nc.scalar.activation(shared.c1_s[:, 0], wq_raw[:, 0], ACT.Copy).then_inc(shared.c1_high, 1)
                        act.wait_ge(shared.w1_loaded, 16)
                    if drain0 in range(1, 1 + shared.W1_EARLY):
                        nc.scalar.activation(shared.w1_s[:, drain0 - 1, 0], wq_raw[:, drain0],
                                             ACT.Copy).then_inc(shared.w1_high, 1)
                    if drain0 == 1 + shared.W1_EARLY:
                        act.wait_ge(shared.c2_loaded, 16)
                        nc.scalar.activation(shared.c2_s, c2_raw, ACT.Copy).then_inc(shared.c2_high, 1)
                    if drain1 == ROOT_AT:
                        front.root(act, 0)
                    if drain1 in range(XT_AT, XT_AT + KC):
                        front.high_xT(act, 0, drain1 - XT_AT, front_banks)
                    if drain1 == T_AT:
                        front.high_t(act, 0, front_banks)

            def store_x1(T):
                act.wait_ge(acc_read, TC * T)
                act.dma_start(x1_d[T - 1], x1[:]).then_inc(x1_stored, 16)

            rounds(act, body)
            store_x1(NT)

        @block.vector
        def _(dve):
            def maximum(batch):
                dve.wait_ge(s_done, batch + 1)
                wait(dve, e_done, HALVES * batch)
                nc.vector.tensor_reduce(negmax[:], s_ps[:], AXIS.X, ALU.max, negate=True).then_inc(max_done, 1)

            def low_o(T, g, j, b, c):
                if not (b if j else c):
                    return
                og, oj = (earlier(T, g, 1)[1], j - 1) if j else (earlier(T, g, 2)[1], HG - 1)
                dve.wait_ge(o_high, HG * (GROUPS * T + g - 1) + j)
                part = o[:, og % 2, :, :, oj * L:(oj + 1) * L]
                nc.vector.tensor_tensor(part[:, 1], o_ps[:].rearrange("p (h t) -> p h t", h=HG), part[:, 0],
                                        ALU.subtract).then_inc(o_low, 1)

            def body(T, g, a, b, c):
                u = GROUPS * T + g
                steady = a and b and c
                for j in range(HG):
                    batch = HG * (u - 1) + j
                    if b and (steady or j == 0):
                        maximum(batch)
                    if steady:
                        low_o(T, g, j, b, c)
                    if b:
                        wait(dve, pT_done, batch)
                        for half in range(HALVES):
                            number = HALVES * batch + half
                            rows = slice(2 * half, 2 * half + 2)
                            dve.wait_ge(e_done, number + 1)
                            nc.vector.reciprocal(inverse[:, rows], total[:, rows]).then_inc(inverse_done, 1)
                            dve.wait_ge(inverse_done, number + 1)
                            nc.vector.tensor_tensor(prob[:, rows], e[:, rows],
                                                    inverse[:, rows].unsqueeze(2).to_broadcast([P, 2, KEYS]),
                                                    ALU.mult).then_inc(prob_done, 1)
                    if not steady:
                        low_o(T, g, j, b, c)
                        if b and j < HG - 1:
                            maximum(batch + 1)
                    if b:
                        dve.wait_ge(pT_high, batch + 1)
                        nc.vector.tensor_tensor(probT[:, 1], pT_ps[:], probT[:, 0], ALU.subtract).then_inc(pT_low, 1)
                    drain0, drain1 = drain_slots(T, g, j)
                    if drain0 == HG - 1:
                        dve.wait_ge(shared.c2_high, 1)
                        nc.vector.tensor_tensor(shared.c2_s[P // 2:P], c2_raw[P // 2:P], shared.c2_s[P // 2:P],
                                                ALU.subtract).then_inc(shared.c2_low, 1)
                    if drain1 == ROOT_AT:
                        for chunk in range(TC):
                            front.statistics(dve, 0, chunk)
                        front.variance(dve, 0)
                        front.invert(dve, 0)
                        for chunk in range(TC):
                            front.apply(dve, 0, chunk)
                    if drain1 in range(XT_AT, XT_AT + KC):
                        front.low_xT(dve, 0, drain1 - XT_AT, front_banks)
                    if drain1 == T_AT:
                        front.low_t(dve, 0, front_banks)
                if c and g == 1 and not (isinstance(T, int) and T == 0):
                    dve.wait_ge(x_loaded, 16 * T)
                    for i in range(TC):
                        if i < TC - 1:
                            dve.wait_ge(acc_done, (TC - 1) * (T - 1) + i + 1)
                        else:
                            dve.wait_ge(wo_done, HG * (u - 1))
                        nc.vector.tensor_tensor(x1[:, i], x1[:, i], acc[i][:], ALU.add).then_inc(acc_read, 1)

            rounds(dve, body)

        @block.tensor
        def _(pe):
            def scores(bT, bg, j):
                step = GROUPS * bT + bg
                if j == 0:
                    pe.wait_ge(q_copied, HG * (step + 1))
                    pe.wait_ge(k_loaded[bg % 2], 16 * (2 * bT + bg // 2 + 1))
                wait(pe, e_done, HALVES * (TB * step + j))
                for i in range(4):
                    last = nc.tensor.matmul(s_ps[:, i], q[:, bg % 2, j, 2 * i:2 * i + 2].rearrange("p h t -> p (h t)"),
                                            k[:, bg % 2, j], start=True, stop=True)
                last.then_inc(s_done, 1)

            def transpose(batch):
                wait(pe, pT_low, batch)
                for i in range(4):
                    if i % 2 == 0:
                        pe.wait_ge(prob_done, HALVES * batch + i // 2 + 1)
                    last = nc.tensor.transpose(pT_ps[:, i * P:(i + 1) * P], prob[:, i], ident[:])
                last.then_inc(pT_done, 1)

            def times_v(bT, bg, j):
                batch = TB * (GROUPS * bT + bg) + j
                pe.wait_ge(pT_low, batch + 1)
                if j == 0:
                    pe.wait_ge(v_loaded[bg % 2], 32 * (2 * bT + bg // 2 + 1))
                wait(pe, o_low, batch)
                three_passes(nc, o_ps[:], [v[:, bg % 2, s, j] for s in range(2)],
                             [probT[:, s] for s in range(2)], True, True).then_inc(pv_done, 1)

            def project_q(T, g, j, chunks):
                u = GROUPS * T + g
                slot = HG * u + j
                if chunks[0] == 0:
                    pe.wait_ge(wq_low, slot + 1)
                    wait(pe, q_copied, slot - 1 if alternating(T, g) else slot)
                    if j == 0 and g % 2 == 0:
                        pe.wait_ge(xT_loaded[g // 2], 32 * (T + 1))
                for i in chunks:
                    last = three_passes(nc, q_bank(T, g, j)[:], [wq_s[:, j % 2, s, i] for s in range(2)],
                                        [xT[g // 2][:, s, i] for s in range(2)], i == 0, i == KC - 1)
                if chunks[-1] == KC - 1:
                    last.then_inc(q_done, 1)

            def project_out(T, g, cg, j, chunks):
                u = GROUPS * T + g
                if chunks[0] == 0:
                    pe.wait_ge(wo_low, HG * (u - 2) + j + 1)
                if j == 0 and cg == 0 and chunks[0] == 0:
                    wait(pe, acc_read, TC * (T if g >= 2 else T - 1))
                for i in chunks:
                    if j == 0 and i == 0:
                        pe.wait_ge(o_low, HG * (u - 1) - 1)
                    if j == 0 and i == TC - 1:
                        pe.wait_ge(o_low, HG * (u - 1))
                    last = three_passes(nc, acc[i][:], [o[:, cg % 2, s, j, i * P:(i + 1) * P] for s in range(2)],
                                        [wo_s[:, j % 2, s] for s in range(2)],
                                        cg == 0 and j == 0, cg == GROUPS - 1 and j == HG - 1)
                    if cg == GROUPS - 1 and j == HG - 1 and i < TC - 1:
                        last.then_inc(acc_done, 1)
                if chunks[-1] == TC - 1:
                    last.then_inc(wo_done, 1)

            def body(T, g, a, b, c):
                u = GROUPS * T + g
                bT, bg = earlier(T, g, 1)
                _, cg = earlier(T, g, 2)
                chunks = list(range(KC))
                SPLIT = 2
                for j in range(HG):
                    batch = HG * (u - 1) + j
                    _, drain1 = drain_slots(T, g, j)
                    if drain1 in range(XT_AT, XT_AT + KC):
                        front.transpose(pe, 0, drain1 - XT_AT, front_banks)
                    if drain1 == T_AT:
                        pe.wait_ge(shared.c1_low, 1)
                        front.project_t(pe, 0, front_banks)
                    if not (a and b and c):
                        if b and j == 0:
                            scores(bT, bg, 0)
                        for part in (chunks[:SPLIT], chunks[SPLIT:]):
                            if a:
                                project_q(T, g, j, part)
                            if c:
                                project_out(T, g, cg, j, part)
                            if b and part[0] == 0:
                                transpose(batch)
                                if j < HG - 1:
                                    scores(bT, bg, j + 1)
                        if b:
                            times_v(bT, bg, j)
                        continue
                    scores(bT, bg, j)
                    project_out(T, g, cg, j, range(TC))
                    project_q(T, g, j, chunks[:1])
                    transpose(batch)
                    project_q(T, g, j, chunks[1:])
                    times_v(bT, bg, j)

            rounds(pe, body)


def feed_forward(nc, shared, front, x1_d, w1, w2, out):
    with ExitStack() as stack:
        n = Names(nc, stack, "ff")
        ident, xT, t_s, c2_s = shared.ident, front.xT, front.t_s, shared.c2_s
        EARLY_W1 = shared.W1_EARLY
        w2_s = n.sb("w2_s", [P, NI, 2, D], F32R)
        ident_bf = n.sb("ident_bf", [P, P], BF16)
        leader_f = n.sb("leader_f", [P, P])
        leader = n.sb("leader", [P, P], BF16)
        w1_later = n.sb("w1_s", [P, NI - EARLY_W1, 2, KC, P], F32R)
        raw = n.sb("raw", [P, 2, D])
        x_res = raw
        top = n.sb("top", [P, 2, FB])
        chosen = n.sb("chosen", [P, TC, INTER], BF16)
        chosenT = n.sb("chosenT", [P, TT], BF16)
        hidden = n.sb("hidden", [P, NI, TT])
        used_s = n.sb("used_s", [P, 2, 2, TT], F32R)
        w1_raw = hidden

        acc = [n.ps(f"acc{c}") for c in range(TC)]
        h_ps = [n.ps(f"h{i}") for i in range(2)]
        m_ps = [n.ps(f"m{i}") for i in range(2)]
        cT_ps = m_ps[0][:].bitcast(BF16)[:, 0:TT]

        ident_bf_done = n.sem("ident_bf_done")
        leader_step = n.sem("leader_step")
        leader_done = n.sem("leader_done")
        w1_high, w1_low = shared.w1_high, shared.w1_low
        w2_high = n.sem("w2_high")
        w2_low = n.sem("w2_low")
        score_done = n.sem("score_done")
        top_done = n.sem("top_done")
        chosen_done = n.sem("chosen_done")
        h_done = n.sem("h_done")
        relu_done = n.sem("relu_done")
        cT_done = n.sem("cT_done")
        cT_copied = n.sem("cT_copied")
        mask_done = n.sem("mask_done")
        used_done = n.sem("used_done")
        used_high = n.sem("used_high")
        used_low = n.sem("used_low")
        out_done = n.sem("out_done")
        y_done = n.sem("y_done")
        w2_loaded = [n.sem(f"w2_loaded{i}") for i in range(2)]
        x_res_loaded = [n.sem(f"x_res_loaded{i}") for i in range(2)]
        acc_done = n.sem("acc_done")
        y_last_stored = n.sem("y_last_stored")
        y_stored = [n.sem(f"y_stored{i}") for i in range(2)]

        W1_LOADS = [3, 4, 5, 7, 10, NI]
        w1_loaded = [n.sem(f"w1_loaded{i}") for i in range(len(W1_LOADS) - 1)]
        EARLY, ROOT_AT, XT_AT, T_AT = 10, 4, 7, 12
        AHEAD = EARLY_W1
        BEHIND = 6
        X1_AT = 8

        def w1_parts(i, c):
            chunk = shared.w1_s[:, i] if i < EARLY_W1 else w1_later[:, i - EARLY_W1]
            return [chunk[:, s, c] for s in range(2)]

        def w1_load(i):
            return max(m for m in range(len(W1_LOADS) - 1) if W1_LOADS[m] <= i)

        def tiles(engine, body):
            body(0, True, False)
            with engine.Fori(1, NT - 1) as T:
                body(T, False, False)
            body(NT - 1, False, True)

        block = stack.enter_context(nc.Block())

        @block.sync
        def _(sp):
            def next_tile(T):
                sp.wait_ge(front.xT_done, KC * (T + 1))
                front.load(sp, T + 1)

            for m in range(len(W1_LOADS) - 1):
                at = slice(W1_LOADS[m], W1_LOADS[m + 1])
                sp.dma_start(w1_raw[:, at].rearrange("p i n -> p (i n)"),
                             w1[:, at].rearrange("p i c n -> p (i c n)")).then_inc(w1_loaded[m], 16)
            for i in range(NI):
                if i == 2:
                    next_tile(0)
                if i == X1_AT:
                    sp.wait_ge(shared.x1_stored, 16 * NT)
                wait(sp, w2_low, i - 1)
                sp.dma_start(raw[:, i % 2], w2[i * P:(i + 1) * P]).then_inc(w2_loaded[i % 2], 16)
            sp.wait_ge(w2_low, NI)

            def residual(T, c):
                if c < 2:
                    wait(sp, y_stored[c], 32 * T)
                else:
                    sp.wait_ge(y_stored[c % 2], 32 * T + 16)
                sp.dma_start(x_res[:, c % 2], x1_d[T, :, c]).then_inc(x_res_loaded[c % 2], 16)

            def store(T, c):
                sp.wait_ge(y_done, TC * T + c + 1)
                sp.dma_start(out[T, :, c], x_res[:, c % 2]).then_inc(y_stored[c % 2], 16)

            def body(T, first, last):
                if last:
                    sp.wait_ge(front.xT_done, KC * NT)
                    front.load(sp, T)
                    for c in range(TC):
                        sp.wait_ge(y_done, TC * T + c + 1)
                        sp.dma_start(out[T, :, c], front.x[:, c]).then_inc(y_last_stored, 16)
                    return
                if not first:
                    next_tile(T)
                residual(T, 0)
                residual(T, 1)
                for c in range(TC):
                    store(T, c)
                    if c < 2:
                        residual(T, c + 2)

            tiles(sp, body)
            for i in range(2):
                sp.wait_ge(y_stored[i], 32 * (NT - 1))
            sp.wait_ge(y_last_stored, 16 * TC)

        @block.gpsimd
        def _(pool):
            nc.gpsimd.memset(leader_f[:], -1.0).then_inc(leader_step, 1)
            pool.wait_ge(leader_step, 1)
            nc.gpsimd.affine_select(out=leader_f[:], in_=leader_f[:], compare_op=ALU.is_gt, fill=0.0, base=0,
                                    pattern=[[1, P]], channel_multiplier=-1).then_inc(leader_step, 1)
            pool.wait_ge(leader_step, 2)
            nc.gpsimd.affine_select(out=leader_f[:].rearrange("p (b s) -> p b s", s=SPARSE),
                                    in_=leader_f[:].rearrange("p (b s) -> p b s", s=SPARSE),
                                    compare_op=ALU.is_ge, fill=0.0, base=0,
                                    pattern=[[-SPARSE, P // SPARSE], [0, SPARSE]],
                                    channel_multiplier=1).then_inc(leader_step, 1)
            pool.wait_ge(leader_step, 3)
            nc.gpsimd.affine_select(out=leader_f[:], in_=leader_f[:], compare_op=ALU.not_equal, fill=1.0, base=0,
                                    pattern=[[-1, P]], channel_multiplier=1).then_inc(leader_step, 1)

            def low_w1(i):
                pool.wait_ge(w1_high, i + 1)
                nc.gpsimd.tensor_tensor(w1_later[:, i - EARLY_W1, 1], w1_raw[:, i].rearrange("p (c n) -> p c n", c=KC),
                                        w1_later[:, i - EARLY_W1, 0], ALU.subtract).then_inc(w1_low, 1)

            def low_w2(i):
                pool.wait_ge(w2_high, i + 1)
                nc.gpsimd.tensor_tensor(w2_s[:, i, 1], raw[:, i % 2], w2_s[:, i, 0], ALU.subtract).then_inc(w2_low, 1)

            for i in range(NI):
                if i + AHEAD < NI:
                    low_w1(i + AHEAD)
                if i >= BEHIND:
                    low_w2(i - BEHIND)
            for i in range(NI - BEHIND, NI):
                low_w2(i)

        @block.scalar
        def _(act):
            def high_w1(i):
                act.wait_ge(w1_loaded[w1_load(i)], 16)
                nc.scalar.activation(w1_later[:, i - EARLY_W1, 0], w1_raw[:, i].rearrange("p (c n) -> p c n", c=KC),
                                     ACT.Copy).then_inc(w1_high, 1)

            def high_w2(i):
                act.wait_ge(w2_loaded[i % 2], 16 * (i // 2 + 1))
                nc.scalar.activation(w2_s[:, i, 0], raw[:, i % 2], ACT.Copy).then_inc(w2_high, 1)

            def copy_chosenT(T, i):
                number = NI * T + i
                act.wait_ge(cT_done, number + 1)
                wait(act, mask_done, number)
                nc.scalar.activation(chosenT[:], cT_ps, ACT.Copy).then_inc(cT_copied, 1)

            def high_used(T, i):
                number = NI * T + i
                act.wait_ge(used_done, number + 1)
                wait(act, out_done, number - 1)
                nc.scalar.activation(used_s[:, i % 2, 0], hidden[:, i], ACT.Copy).then_inc(used_high, 1)

            def body(T, first, last):
                for i in range(NI):
                    number = NI * T + i
                    if first:
                        if i + AHEAD < NI:
                            high_w1(i + AHEAD)
                        if i >= BEHIND:
                            high_w2(i - BEHIND)
                    act.wait_ge(h_done, number + 1)
                    wait(act, used_low, number - NI + 1)
                    nc.scalar.activation(hidden[:, i], h_ps[i % 2][:], ACT.Relu).then_inc(relu_done, 1)
                    if i == EARLY:
                        copy_chosenT(T, 0)
                    if i == EARLY + 1:
                        copy_chosenT(T, 1)
                        high_used(T, 0)
                    if i == EARLY + 2:
                        high_used(T, 1)
                for i in range(NI):
                    if i + 2 < NI:
                        copy_chosenT(T, i + 2)
                        high_used(T, i + 2)
                    if first and i < BEHIND:
                        high_w2(NI - BEHIND + i)
                    if last:
                        continue
                    if i == ROOT_AT:
                        front.root(act, T + 1)
                    if i in range(XT_AT, XT_AT + KC):
                        front.high_xT(act, T + 1, i - XT_AT, h_ps)
                    if i == T_AT:
                        act.wait_ge(score_done, TC * FQ * (T + 1))
                        front.high_t(act, T + 1, h_ps)

            tiles(act, body)

        @block.vector
        def _(dve):
            def choose(T, m):
                c, f = m // FQ, m % FQ
                number = TC * FQ * T + m
                scores = m_ps[m % 2][:, 0:FN].rearrange("p (b s) -> p b s", s=SPARSE)
                dve.wait_ge(score_done, number + 1)
                nc.vector.tensor_reduce(top[:, m % 2], scores, AXIS.X, ALU.max).then_inc(top_done, 1)
                dve.wait_ge(top_done, number + 1)
                if m == 0:
                    wait(dve, cT_done, NI * T)
                nc.vector.tensor_tensor(chosen[:, c, f * FN:(f + 1) * FN].rearrange("p (b s) -> p b s", s=SPARSE), scores,
                                        top[:, m % 2].unsqueeze(2).to_broadcast([P, FB, SPARSE]),
                                        ALU.is_equal).then_inc(chosen_done, 1)

            def use(T, i):
                number = NI * T + i
                dve.wait_ge(relu_done, NI * T + max(i, EARLY + i + 1 if i < 2 else NI))
                dve.wait_ge(mask_done, number + 1)
                nc.vector.scalar_tensor_tensor(hidden[:, i], m_ps[1][:], 0.0, hidden[:, i], ALU.max,
                                               ALU.mult).then_inc(used_done, 1)
                dve.wait_ge(used_high, number + 1)
                nc.vector.tensor_tensor(used_s[:, i % 2, 1], hidden[:, i], used_s[:, i % 2, 0],
                                        ALU.subtract).then_inc(used_low, 1)

            def add_x(T, chunks):
                for c in chunks:
                    dve.wait_ge(x_res_loaded[c % 2], 32 * T + 16 * (c // 2 + 1))
                    nc.vector.tensor_tensor(x_res[:, c % 2], x_res[:, c % 2], acc[c][:], ALU.add).then_inc(y_done, 1)

            def body(T, first, last):
                for i in range(NI):
                    if i < TC * FQ // 2:
                        choose(T, 2 * i)
                        choose(T, 2 * i + 1)
                    if i == TC * FQ // 2 and not first:
                        add_x(T - 1, (2, 3))
                    if i in (EARLY + 1, EARLY + 2):
                        use(T, i - EARLY - 1)
                for i in range(NI):
                    if i + 2 < NI:
                        use(T, i + 2)
                    if last:
                        continue
                    if i < TC:
                        front.statistics(dve, T + 1, i)
                    if i == ROOT_AT - 1:
                        front.variance(dve, T + 1)
                    if i == ROOT_AT + 1:
                        front.invert(dve, T + 1)
                    if i in (ROOT_AT + 1, ROOT_AT + 2):
                        for c in range(2 * (i - ROOT_AT - 1), 2 * (i - ROOT_AT)):
                            front.apply(dve, T + 1, c)
                    if i in range(XT_AT, XT_AT + KC):
                        front.low_xT(dve, T + 1, i - XT_AT, h_ps)
                    if i == T_AT:
                        front.low_t(dve, T + 1, h_ps)
                if last:
                    dve.wait_ge(front.loaded, 16 * (NT + 1))
                    for c in range(TC):
                        dve.wait_ge(acc_done, c + 1)
                        nc.vector.tensor_tensor(front.x[:, c], front.x[:, c], acc[c][:], ALU.add).then_inc(y_done, 1)
                else:
                    dve.wait_ge(out_done, NI * (T + 1))
                    add_x(T, (0, 1))

            nc.vector.tensor_copy(ident_bf[:], ident[:]).then_inc(ident_bf_done, 1)
            dve.wait_ge(leader_step, 4)
            nc.vector.tensor_copy(leader[:], leader_f[:]).then_inc(leader_done, 1)
            tiles(dve, body)

        @block.tensor
        def _(pe):
            def score(T, m):
                c, f = m // FQ, m % FQ
                number = TC * FQ * T + m
                wait(pe, chosen_done, number - 1)
                nc.tensor.matmul(m_ps[m % 2][:, 0:FN], t_s[:, c * P:(c + 1) * P], c2_s[:, f * FN:(f + 1) * FN],
                                 start=True, stop=True).then_inc(score_done, 1)

            def transpose_chosen(T, i):
                number = NI * T + i
                wait(pe, cT_copied, number)
                for c in range(TC):
                    last = nc.tensor.transpose(cT_ps[:, c * P:(c + 1) * P], chosen[:, c, i * P:(i + 1) * P], ident_bf[:])
                last.then_inc(cT_done, 1)

            def mask(T, i):
                number = NI * T + i
                pe.wait_ge(cT_copied, number + 1)
                wait(pe, used_done, number)
                nc.tensor.matmul(m_ps[1][:], leader[:], chosenT[:], start=True, stop=True).then_inc(mask_done, 1)

            def down(T, i, first, last):
                number = NI * T + i
                pe.wait_ge(used_low, number + 1)
                if first:
                    pe.wait_ge(w2_low, i + 1)
                if i == 0:
                    wait(pe, y_done, TC * T)
                for c in range(TC):
                    last_mm = three_passes(nc, acc[c][:], [used_s[:, i % 2, s, c * P:(c + 1) * P] for s in range(2)],
                                        [w2_s[:, i, s] for s in range(2)], i == 0, i == NI - 1)
                    if last and i == NI - 1:
                        last_mm.then_inc(acc_done, 1)
                if not (last and i == NI - 1):
                    last_mm.then_inc(out_done, 1)

            def body(T, first, last):
                pe.wait_ge(front.t_low, 2 * (T + 1))
                wait(pe, used_done, NI * T)
                for i in range(NI):
                    number = NI * T + i
                    if first:
                        pe.wait_ge(w1_low, i + 1)
                    wait(pe, relu_done, number - 1)
                    for half in range(2):
                        if i < TC * FQ // 2:
                            score(T, 2 * i + half)
                        for c in range(KC // 2 * half, KC // 2 * (half + 1)):
                            last_mm = three_passes(nc, h_ps[i % 2][:], w1_parts(i, c),
                                                   [xT[:, s, c] for s in range(2)], c == 0, c == KC - 1)
                    last_mm.then_inc(h_done, 1)
                    if i == EARLY:
                        pe.wait_ge(chosen_done, TC * FQ * (T + 1))
                        if first:
                            pe.wait_ge(ident_bf_done, 1)
                        transpose_chosen(T, 0)
                    if i == EARLY + 1:
                        if first:
                            pe.wait_ge(leader_done, 1)
                        mask(T, 0)
                        transpose_chosen(T, 1)
                    if i == EARLY + 2:
                        mask(T, 1)
                for i in range(NI):
                    if i + 2 < NI:
                        transpose_chosen(T, i + 2)
                    down(T, i, first, last)
                    if not last:
                        if i in range(XT_AT, XT_AT + KC):
                            front.transpose(pe, T + 1, i - XT_AT, h_ps)
                        if i == T_AT:
                            front.project_t(pe, T + 1, h_ps)
                    if i + 2 < NI:
                        mask(T, i + 2)

            tiles(pe, body)


def build(nc, x, ctxT, wq, wk, wv, wo, c1, c2, w1, w2, out):
    kT_d = nc.dram_tensor("kT_d", [GROUPS, P, NKT, KT * KEYS], F32, kind="Internal").ap()
    v_d = nc.dram_tensor("v_d", [GROUPS, 2, P, NKT, KT, DH], F32, kind="Internal").ap()
    xnT_d = nc.dram_tensor("xnT_d", [2, NT, P, KC, 2, KT, L], F32, kind="Internal").ap()
    x1_d = nc.dram_tensor("x1_d", [NT, P, TC, D], F32, kind="Internal").ap()
    with ExitStack() as stack:
        shared = Shared(nc, stack)
        front = Front(nc, stack, shared, x1_d)
        with nc.sbuf_tensor("wq_raw", [P, shared.RAW, KC, DH], F32) as wq_raw:
            project_keys_values(nc, shared, wq_raw, x, ctxT, wq, wk, wv, kT_d, v_d, xnT_d)
            attend(nc, shared, wq_raw, front, x, wq, wo, c1, c2, w1, kT_d, v_d, xnT_d, x1_d)
        feed_forward(nc, shared, front, x1_d, w1, w2, out)


def kernel(x, ctx_4096, L0_xattn_Wq, L0_xattn_Wk, L0_xattn_Wv, L0_xattn_Wo,
           L0_ffn_c1_w, L0_ffn_c2_w, L0_ffn_w1, L0_ffn_w2t):
    import numpy as np
    import concourse.bacc as bacc
    from concourse.bass_utils import run_bass_kernel_spmd

    x, ctx, wq, wk, wv, wo, c1, c2, w1, w2 = (np.asarray(a) for a in (
        x, ctx_4096, L0_xattn_Wq, L0_xattn_Wk, L0_xattn_Wv, L0_xattn_Wo,
        L0_ffn_c1_w, L0_ffn_c2_w, L0_ffn_w1, L0_ffn_w2t))
    c1_at = np.zeros((P, KC, P), c1.dtype)
    c2_at = np.zeros((P, INTER), c2.dtype)
    for r in range(P // RANK_STEP):
        at = slice(r * RANK_STEP, r * RANK_STEP + RANK)
        c1_at[:, :, at] = c1.reshape(RANK, KC, P).transpose(2, 1, 0)
        c2_at[at] = c2.T
    arrays = {
        "x": x.reshape(TOKENS, D),
        "ctxT": ctx.reshape(TOKENS, D).T,
        "wq": wq.reshape(KC, P, HEADS, DH).transpose(1, 2, 0, 3),
        "wk": wk, "wv": wv, "wo": wo,
        "c1": c1_at, "c2": c2_at,
        "w1": w1.reshape(NI, P, KC, P).transpose(3, 0, 2, 1),
        "w2": w2,
    }
    arrays = {name: np.ascontiguousarray(a) for name, a in arrays.items()}
    nc = bacc.Bacc("TRN2", target_bir_lowering=False, num_devices=1)
    aps = [nc.dram_tensor(name, list(a.shape), mybir.dt.from_np(a.dtype), kind="ExternalInput").ap()
           for name, a in arrays.items()]
    out = nc.dram_tensor("out", [TOKENS, D], F32, kind="ExternalOutput").ap()
    build(nc, *aps, out.rearrange("(t c p) d -> t p c d", c=TC, p=P))
    result = run_bass_kernel_spmd(nc, [arrays], core_ids=[0]).results[0]["out"]
    return result.reshape(B, L, D)
```
